# Optimizing a Trainium2 kernel written in Bass

```python
import numpy as np
import jax
import jax.numpy as jnp

def _softmax(x, axis=-1):
    return jax.nn.softmax(x, axis=axis)

def _gelu(x):
    return jax.nn.gelu(x, approximate=True)

def _silu(x):
    return jax.nn.silu(x)

def _sigmoid(x):
    return jax.nn.sigmoid(x)

def _layernorm(x, axis=-1, eps=1e-05):
    m = jnp.mean(x, axis=axis, keepdims=True)
    v = jnp.var(x, axis=axis, keepdims=True)
    return (x - m) / jnp.sqrt(v + eps)

def _scatter_add(tgt, idx, src, axis=0):
    return tgt.at[idx].add(src)

def _segment_sum(src, seg, n):
    return jax.ops.segment_sum(src, seg, n)
kernel_name = 'mk_adaln_ffn_d1_seqx_r8_a5885d'

def setup_inputs(seed: int=0):
    np.random.seed(seed)
    _w = jnp.asarray

    def _rec_inputs():
        import jax
        import jax.numpy as jnp
        _rk = jax.random.key(seed)
        x = -0.0003929 + 0.9999 * jax.random.normal(jax.random.fold_in(_rk, 1), (128, 32, 512), jnp.float32)
        _lenS = 32 - jax.random.randint(jax.random.fold_in(_rk, 7), (128,), 0, max(1, 32 // 4) + 1, jnp.int32)
        _lenS2 = 32 - jax.random.randint(jax.random.fold_in(_rk, 8), (128,), 0, max(1, 32 // 4) + 1, jnp.int32)
        itok_B_78_3631 = jax.random.randint(jax.random.fold_in(_rk, 11), (128,), 78, 454, jnp.int32)
        return (x, itok_B_78_3631)
    x, itok_B_78_3631 = _rec_inputs()

    def _L0_cond_setup():
        import math
        import jax, jax.numpy as jnp
        import numpy as np
        B, H, N, L = (16, 32, 64, 512)
        DT_MIN, DT_MAX = (0.001, 0.1)

        def _get_kernel(log_dt, C, log_A_real, A_imag, length):
            dt = jnp.exp(log_dt)
            Cc = C[..., 0] + 1j * C[..., 1]
            A = -jnp.exp(log_A_real) + 1j * A_imag
            dtA = A * dt[:, None]
            Ct = Cc * (jnp.exp(dtA) - 1.0) / A
            P = dtA[:, :, None] * jnp.arange(length, dtype=jnp.float32)
            K = 2.0 * jnp.einsum('hn,hnl->hl', Ct, jnp.exp(P)).real
            return K
        key = jax.random.key(seed)
        ks = jax.random.split(key, 5)
        u = jax.random.normal(ks[0], (B, H, L), dtype=jnp.float32)
        log_dt = jax.random.uniform(ks[1], (H,), dtype=jnp.float32) * (math.log(DT_MAX) - math.log(DT_MIN)) + math.log(DT_MIN)
        C = jax.random.normal(ks[2], (H, N, 2), dtype=jnp.float32)
        log_A_real = jnp.log(0.5 * jnp.ones((H, N), dtype=jnp.float32))
        A_imag = math.pi * jnp.broadcast_to(jnp.arange(N, dtype=jnp.float32), (H, N))
        D = jax.random.normal(ks[3], (H,), dtype=jnp.float32)
        length = jax.random.randint(ks[4], (B,), 1, L + 1, dtype=jnp.int32)
        return {'u': u, 'log_dt': log_dt, 'C': C, 'log_A_real': log_A_real, 'A_imag': A_imag, 'D': D, 'length': length}
    _L0_cond_all = _L0_cond_setup()
    _L0_cond_in = {k: v for k, v in _L0_cond_all.items() if k in ('log_dt', 'C', 'log_A_real', 'A_imag', 'D')}
    del _L0_cond_all

    def _L0_ffn_setup():
        import jax, jax.numpy as jnp
        import numpy as np
        H = 512
        I = 256
        E = 16
        TOPK = 4
        SI = 256
        key = jax.random.key(seed)
        ks = jax.random.split(key, 9)
        s = 0.02
        return {'hidden_states': jax.random.normal(ks[0], (2, 256, H), dtype=jnp.float32), 'gate_w': jax.random.normal(ks[1], (E, H), dtype=jnp.float32) * s, 'bias': jnp.zeros((E,), dtype=jnp.float32), 'Wg': jax.random.normal(ks[2], (E, I, H), dtype=jnp.float32) * s, 'Wu': jax.random.normal(ks[3], (E, I, H), dtype=jnp.float32) * s, 'Wd': jax.random.normal(ks[4], (E, H, I), dtype=jnp.float32) * s, 'Sg': jax.random.normal(ks[5], (SI, H), dtype=jnp.float32) * s, 'Su': jax.random.normal(ks[6], (SI, H), dtype=jnp.float32) * s, 'Sd': jax.random.normal(ks[7], (H, SI), dtype=jnp.float32) * s}
    _L0_ffn_all = _L0_ffn_setup()
    _L0_ffn_in = {k: v for k, v in _L0_ffn_all.items() if k in ('gate_w', 'bias', 'Wg', 'Wu', 'Wd', 'Sg', 'Su', 'Sd')}
    del _L0_ffn_all
    return {'x': x, 'itok_B_78_3631': itok_B_78_3631, 'L0_cond_log_dt': _L0_cond_in['log_dt'], 'L0_cond_C': _L0_cond_in['C'], 'L0_cond_log_A_real': _L0_cond_in['log_A_real'], 'L0_cond_A_imag': _L0_cond_in['A_imag'], 'L0_cond_D': _L0_cond_in['D'], 'L0_ffn_gate_w': _L0_ffn_in['gate_w'], 'L0_ffn_bias': _L0_ffn_in['bias'], 'L0_ffn_Wg': _L0_ffn_in['Wg'], 'L0_ffn_Wu': _L0_ffn_in['Wu'], 'L0_ffn_Wd': _L0_ffn_in['Wd'], 'L0_ffn_Sg': _L0_ffn_in['Sg'], 'L0_ffn_Su': _L0_ffn_in['Su'], 'L0_ffn_Sd': _L0_ffn_in['Sd']}

def reference(x, itok_B_78_3631, L0_cond_log_dt, L0_cond_C, L0_cond_log_A_real, L0_cond_A_imag, L0_cond_D, L0_ffn_gate_w, L0_ffn_bias, L0_ffn_Wg, L0_ffn_Wu, L0_ffn_Wd, L0_ffn_Sg, L0_ffn_Su, L0_ffn_Sd):
    import jax
    import jax.numpy as jnp

    def _L0_cond_ref(u, log_dt, C, log_A_real, A_imag, D, length):
        import math
        import jax, jax.numpy as jnp
        import numpy as np
        B, H, N, L = (16, 32, 64, 512)
        DT_MIN, DT_MAX = (0.001, 0.1)

        def _get_kernel(log_dt, C, log_A_real, A_imag, length):
            dt = jnp.exp(log_dt)
            Cc = C[..., 0] + 1j * C[..., 1]
            A = -jnp.exp(log_A_real) + 1j * A_imag
            dtA = A * dt[:, None]
            Ct = Cc * (jnp.exp(dtA) - 1.0) / A
            P = dtA[:, :, None] * jnp.arange(length, dtype=jnp.float32)
            K = 2.0 * jnp.einsum('hn,hnl->hl', Ct, jnp.exp(P)).real
            return K
        Bq, Hq, Lq = u.shape
        K = _get_kernel(log_dt, C, log_A_real, A_imag, Lq)
        n = 2 * Lq
        kf = jnp.fft.rfft(K, n=n)
        uf = jnp.fft.rfft(u, n=n)
        y = jnp.fft.irfft(uf * kf[None], n=n)[..., :Lq]
        y = y + u * D[:, None]
        mask = (jnp.arange(Lq)[None, :] < length[:, None]).astype(u.dtype)
        return y * mask[:, None, :]

    def _L0_ffn_ref(hidden_states, gate_w, bias, Wg, Wu, Wd, Sg, Su, Sd):
        import jax, jax.numpy as jnp
        import numpy as np
        H = 512
        I = 256
        E = 16
        TOPK = 4
        SI = 256
        orig_shape = hidden_states.shape
        x = hidden_states.reshape(-1, orig_shape[-1])
        scores = jax.nn.sigmoid(x @ gate_w.T) + bias
        topk_w, topk_idx = jax.lax.top_k(scores, TOPK)
        topk_w = topk_w / (jnp.sum(topk_w, axis=-1, keepdims=True) + 1e-20)
        cw = jnp.sum(jax.nn.one_hot(topk_idx, E, dtype=x.dtype) * topk_w[..., None], axis=1)
        g = jnp.einsum('th,eih->eti', x, Wg)
        u = jnp.einsum('th,eih->eti', x, Wu)
        z = jax.nn.silu(g) * u
        zw = z * cw.T[:, :, None]
        out = jnp.einsum('eti,ehi->th', zw, Wd)
        out = out + jax.nn.silu(x @ Sg.T) * (x @ Su.T) @ Sd.T
        return out.reshape(orig_shape)
    x = x + _L0_ffn_ref(_L0_cond_ref(x, L0_cond_log_dt, L0_cond_C, L0_cond_log_A_real, L0_cond_A_imag, L0_cond_D, itok_B_78_3631), L0_ffn_gate_w, L0_ffn_bias, L0_ffn_Wg, L0_ffn_Wu, L0_ffn_Wd, L0_ffn_Sg, L0_ffn_Su, L0_ffn_Sd)
    return x

_drawn_inputs = setup_inputs


def setup_inputs(seed=0):
    import zlib

    import numpy as np

    out = dict(_drawn_inputs(seed))
    spreads = {'L0_cond_log_A_real': (-0.6931471824645996, 0.6), 'L0_ffn_bias': (0.0, 0.272)}
    factors = {}
    for name, (base, spread) in spreads.items():
        noise = np.random.default_rng([zlib.crc32(name.encode()), seed]).standard_normal(out[name].shape)
        drawn = base * np.exp(spread * noise) if base else spread * noise
        out[name] = jnp.asarray(drawn.astype(out[name].dtype))
    for name, factor in factors.items():
        out[name] = (out[name] * factor).astype(out[name].dtype)
    return out
```

```python
from contextlib import ExitStack

import concourse.bass as bass
from concourse import mybir

P = 128
F32 = mybir.dt.float32
I32 = mybir.dt.int32
U32 = mybir.dt.uint32
ALU = mybir.AluOpType
ACT = mybir.ActivationFunctionType

B, H, L = 128, 32, 512
N = 64
E, I, TOPK = 16, 256, 4
KT = L // P
IT = I // P
VLEN, ULEN = 32, 16
KPITCH = 640
GH = 4
NG = H // GH

TWO_PI = 6.283185307179586
C1, C2 = 6.28125, 0.00193500518798828125
C3 = TWO_PI - C1 - C2
LN2_HI, LN2_LO = 0.693359375, -2.12194440054690583e-4
ROUND = 12582912.0


class Count:

    def __init__(self, sem):
        self.sem, self.n = sem, 0

    def by(self, instruction, k=1):
        instruction.then_inc(self.sem, k)
        self.n += k
        return self.sem, self.n


def wait(engine, *marks):
    for sem, n in marks:
        engine.wait_ge(sem, n)


def build(nc, x, xT, lens, log_dt, c_re, c_im, log_a, a_im, d_skip, gate_w, bias, wg, wu, wd, sg, su, sd, out, kpad):
    with ExitStack() as ctx:
        def sb(name, shape, dt=F32):
            return ctx.enter_context(nc.sbuf_tensor(name, shape, dt))

        def count(name):
            return Count(ctx.enter_context(nc.semaphore(name)))

        banks = ctx.enter_context(nc.psum_tensor("banks", [P, 8, 512], F32))
        y_t = sb("y_t", [P, KT, H * B])
        arena = sb("arena", [P, H * 512])
        pe, act, dve, pool = nc.tensor, nc.scalar, nc.vector, nc.gpsimd
        c_pe, c_act, c_dve, c_pool = count("c_pe"), count("c_act"), count("c_dve"), count("c_pool")

        def v(ins):
            m = c_dve.by(ins)
            wait(dve, m)
            return m

        par = sb("par", [P, 6, H])
        d_row = sb("d_row", [1, H])
        len_i = sb("len_i", [P, B], I32)
        len_f = sb("len_f", [P, B])
        l_of = sb("l_of", [P, KT], I32)
        l_off = sb("l_off", [P, KT])
        mask = sb("mask", [P, KT, B])
        gate_sb = sb("gate_sb", [P, KT, E])
        bias_sb = sb("bias_sb", [P, E])
        zero = sb("zero", [P, P])
        iota_e = sb("iota_e", [P, E])
        c_par, c_gate = count("c_par"), count("c_gate")
        nc.sync.dma_start(par[:, 0, :], log_dt.partition_broadcast(P)).then_inc(c_par.sem, 16)
        for half in range(2):
            q = slice(N * half, N * half + N)
            for j, src in ((1, log_a), (2, a_im), (3, c_re), (4, c_im)):
                nc.sync.dma_start(par[q, j, :], src).then_inc(c_par.sem, 16)
        c_par.n = 16 * 9
        m_par = (c_par.sem, c_par.n)
        m_d = c_gate.by(nc.scalar.dma_start(d_row[:], d_skip), 16)
        c_gate.by(nc.scalar.dma_start(len_i[:], lens.partition_broadcast(P)), 16)
        c_gate.by(nc.scalar.dma_start(gate_sb[:], gate_w), 16)
        m_gate = c_gate.by(nc.scalar.dma_start(bias_sb[:], bias.partition_broadcast(P)), 16)

        NJ = VLEN + 2 * ULEN + 2
        X0, Y0, S1, SH = VLEN, VLEN + ULEN, NJ - 2, NJ - 1
        l_tab = sb("l_tab", [P, NJ])
        q_tab = sb("q_tab", [P, NJ])
        c_pool.by(pool.iota(l_tab[:, 0:VLEN], [[1, VLEN]], base=0, channel_multiplier=0, allow_small_or_imprecise_dtypes=True))
        c_pool.by(pool.iota(l_tab[:, X0:S1].rearrange("p (k a) -> p k a", k=2), [[0, 2], [VLEN, ULEN]], base=0,
                            channel_multiplier=0, allow_small_or_imprecise_dtypes=True))
        c_pool.by(pool.iota(iota_e[:], [[1, E]], base=0, channel_multiplier=0, allow_small_or_imprecise_dtypes=True))
        m_iota = c_pool.by(pool.iota(l_of[:], [[P, KT]], base=0, channel_multiplier=1))
        dve.memset(l_tab[:, S1:SH], 1.0)
        dve.memset(l_tab[:, SH:NJ], 0.5)
        for lo, quarters in ((0, (1, 1, 2)), (N, (0, 2, 3))):
            q = slice(lo, lo + N)
            dve.memset(q_tab[q, 0:X0], quarters[0] / 4)
            dve.memset(q_tab[q, X0:Y0], quarters[1] / 4)
            dve.memset(q_tab[q, Y0:S1], quarters[2] / 4)
        dve.memset(q_tab[:, S1:NJ], 0.0)
        m_zero = v(dve.memset(zero[:], 0.0))

        sm = sb("sm", [P, 24, 2 * H])
        sm_i = sb("sm_i", [P, 2 * H], I32)

        def accurate_exp(dst, dst_m1, src, w):
            t, k, r, q, s = (sm[:, 16 + j, 0:w] for j in range(5))
            v(dve.tensor_scalar(t, src, -87.0, 88.0, ALU.max, ALU.min))
            v(dve.tensor_scalar(k, t, 1.4426950408889634, ROUND, ALU.mult, ALU.add))
            v(dve.tensor_scalar(k, k, ROUND, None, ALU.subtract))
            v(dve.scalar_tensor_tensor(out=r, in0=k, scalar=-LN2_HI, in1=t, op0=ALU.mult, op1=ALU.add))
            v(dve.scalar_tensor_tensor(out=r, in0=k, scalar=-LN2_LO, in1=r, op0=ALU.mult, op1=ALU.add))
            v(dve.tensor_scalar(q, r, 1 / 5040, None, ALU.mult))
            for c in (1 / 720, 1 / 120, 1 / 24, 1 / 6, 0.5, 1.0):
                v(dve.scalar_tensor_tensor(out=q, in0=q, scalar=c, in1=r, op0=ALU.add, op1=ALU.mult))
            v(dve.tensor_scalar(sm_i[:, 0:w], k, 127.0, 8388608.0, ALU.add, ALU.mult))
            two_k = sm_i[:, 0:w].bitcast(F32)
            v(dve.tensor_tensor(q, q, two_k, ALU.mult))
            if dst_m1 is not None:
                v(dve.tensor_scalar(s, two_k, -1.0, None, ALU.add))
                v(dve.tensor_tensor(dst_m1, q, s, ALU.add))
            return v(dve.tensor_tensor(dst, q, two_k, ALU.add))

        wait(dve, m_par)
        exps = sm[:, 0, :]
        accurate_exp(exps, None, par[:, 0:2, :].rearrange("p a h -> p (a h)"), 2 * H)
        dt, neg_are = sm[:, 0, 0:H], sm[:, 0, H:2 * H]
        aim = par[:, 2, :]
        are, d_re, d_im = sm[:, 1, 0:H], sm[:, 2, 0:H], sm[:, 3, 0:H]
        v(dve.tensor_scalar(are, neg_are, -1.0, None, ALU.mult))
        v(dve.tensor_tensor(d_re, are, dt, ALU.mult))
        v(dve.tensor_tensor(d_im, aim, dt, ALU.mult))

        NM = VLEN + ULEN
        ang = arena[:, 0:H * NJ].rearrange("p (h j) -> p h j", h=H)
        turns = arena[:, H * NJ:2 * H * NJ].rearrange("p (h j) -> p h j", h=H)
        sin = arena[:, 2 * H * NJ:3 * H * NJ].rearrange("p (h j) -> p h j", h=H)
        mag = arena[:, 3 * H * NJ:3 * H * NJ + H * NM].rearrange("p (h j) -> p h j", h=H)
        wide = [P, H, NJ]
        wait(dve, m_iota)
        m_mag = v(dve.tensor_tensor(mag, d_re.unsqueeze(2).to_broadcast([P, H, NM]),
                                    l_tab[:, 0:NM].unsqueeze(1).to_broadcast([P, H, NM]), ALU.mult))
        wait(act, m_mag)
        m_mag = c_act.by(act.activation(mag, mag, ACT.Exp))
        v(dve.tensor_tensor(ang, d_im.unsqueeze(2).to_broadcast(wide), l_tab[:].unsqueeze(1).to_broadcast(wide), ALU.mult))
        q_wide = q_tab[:].unsqueeze(1).to_broadcast(wide)
        v(dve.scalar_tensor_tensor(out=turns, in0=ang, scalar=1 / TWO_PI, in1=q_wide, op0=ALU.mult, op1=ALU.add))
        v(dve.tensor_scalar(turns, turns, ROUND, ROUND, ALU.add, ALU.subtract))
        for part in (C1, C2, C3):
            v(dve.scalar_tensor_tensor(out=ang, in0=turns, scalar=-part, in1=ang, op0=ALU.mult, op1=ALU.add))
        v(dve.scalar_tensor_tensor(out=ang, in0=q_wide, scalar=TWO_PI, in1=ang, op0=ALU.mult, op1=ALU.add))
        m_ang = v(dve.tensor_scalar(ang, ang, 3.1415925, -3.1415925, ALU.min, ALU.max))
        wait(act, m_ang)
        m_sin = c_act.by(act.activation(sin, ang, ACT.Sin))

        ew, em = sm[:, 4, 0:H], sm[:, 5, 0:H]
        accurate_exp(ew, em, d_re, H)
        t0, t1, nr, ni, rd, gr, gi, ctr, cti = (sm[:, 6 + j, 0:H] for j in range(9))
        v(dve.tensor_tensor(t0, are, are, ALU.mult))
        v(dve.tensor_tensor(t1, aim, aim, ALU.mult))
        v(dve.tensor_tensor(t0, t0, t1, ALU.add))
        v(dve.tensor_scalar(t0, t0, 0.5, None, ALU.mult))
        v(dve.reciprocal(rd, t0))
        wait(dve, m_sin)
        s_one, s_half = sin[:, :, S1], sin[:, :, SH]
        v(dve.scalar_tensor_tensor(out=t0, in0=s_half, scalar=2.0, in1=s_half, op0=ALU.mult, op1=ALU.mult))
        v(dve.tensor_tensor(t0, t0, ew, ALU.mult))
        v(dve.tensor_tensor(nr, em, t0, ALU.subtract))
        v(dve.tensor_tensor(ni, ew, s_one, ALU.mult))
        for dst, a, b_, op in ((gr, (nr, are), (ni, aim), ALU.add), (gi, (ni, are), (nr, aim), ALU.subtract)):
            v(dve.tensor_tensor(t0, *a, ALU.mult))
            v(dve.tensor_tensor(t1, *b_, ALU.mult))
            v(dve.tensor_tensor(t0, t0, t1, op))
            v(dve.tensor_tensor(dst, t0, rd, ALU.mult))
        cre, cim = par[:, 3, :], par[:, 4, :]
        for dst, a, b_, op in ((ctr, (cre, gr), (cim, gi), ALU.subtract), (cti, (cre, gi), (cim, gr), ALU.add)):
            v(dve.tensor_tensor(t0, *a, ALU.mult))
            v(dve.tensor_tensor(t1, *b_, ALU.mult))
            v(dve.tensor_tensor(dst, t0, t1, op))
        u_wide = [P, H, ULEN]
        u_x, u_y = sin[:, :, X0:Y0], sin[:, :, Y0:S1]
        v(dve.tensor_tensor(u_x, u_x, ctr.unsqueeze(2).to_broadcast(u_wide), ALU.mult))
        v(dve.tensor_tensor(u_y, u_y, cti.unsqueeze(2).to_broadcast(u_wide), ALU.mult))
        v(dve.tensor_tensor(u_x, u_x, u_y, ALU.add))
        wait(dve, m_mag)
        v(dve.tensor_tensor(u_x, u_x, mag[:, :, VLEN:NM], ALU.mult))
        m_uv = v(dve.tensor_tensor(sin[:, :, 0:VLEN], sin[:, :, 0:VLEN], mag[:, :, 0:VLEN], ALU.mult))

        wait(pe, m_uv)
        for h in range(H):
            k_ps = banks[0:ULEN, 4 + h // 16, (h % 16) * VLEN:(h % 16 + 1) * VLEN]
            mm = pe.matmul(k_ps, u_x[:, h, :], sin[:, h, 0:VLEN], start=True, stop=True)
        m_k = c_pe.by(mm)
        k_sb = sb("k_sb", [ULEN, H, VLEN])
        wait(dve, m_k)
        v(dve.tensor_copy(k_sb[:].rearrange("a (g h) b -> a g (h b)", g=2), banks[0:ULEN, 4:6, :]))
        wait(dve, m_gate)
        m_ksb = v(dve.tensor_tensor(k_sb[0:1, :, 0], k_sb[0:1, :, 0], d_row[:], ALU.add))
        c_kpad = count("c_kpad")
        kh = kpad.tensor
        wait(nc.sync, m_zero)
        c_kpad.by(nc.sync.dma_start(bass.AP(kh, 0, [[KPITCH, H], [1, P - 1]]), zero[0:H, 0:P - 1]), 16)
        wait(nc.sync, m_ksb)
        m_kpad = c_kpad.by(nc.sync.dma_start(bass.AP(kh, P - 1, [[VLEN, ULEN], [KPITCH, H], [1, VLEN]]), k_sb[:]), 16)

        v(dve.tensor_copy(len_f[:], len_i[:]))
        v(dve.tensor_copy(l_off[:], l_of[:]))
        for j in range(KT):
            v(dve.tensor_scalar(mask[:, j, :], len_f[:], l_off[:, j:j + 1], None, ALU.is_gt))

        NR = 2
        taps = sb("taps", [P, NR, GH, 512])
        xin = sb("xin", [P, NR, KT, GH * B])
        c_taps = [count(f"c_taps{i}") for i in range(NR)]
        c_xin = [count(f"c_xin{i}") for i in range(NR)]
        wait(nc.sync, m_kpad)
        used = {}
        evac = {}
        loaded = {}

        def load_group(g):
            r = g % NR
            if g >= NR:
                wait(nc.sync, used[g - NR])
            a = c_xin[r].by(nc.sync.dma_start(xin[:, r], xT[:, :, g * GH * B:(g + 1) * GH * B].rearrange("m p t -> p m t")), 16)
            b_ = c_taps[r].by(nc.sync.dma_start(taps[:, r], bass.AP(kh, KPITCH * GH * g, [[1, P], [KPITCH, GH], [1, 512]])), 16)
            loaded[g] = (a, b_)

        for g in range(NR):
            load_group(g)
        wait(pe, m_gate)
        for h in range(H + 1):
            if h < H:
                g, r = h // GH, (h // GH) % NR
                if h % GH == 0:
                    wait(pe, *loaded[g])
                if h >= 4:
                    wait(pe, evac[h - 4])
                for d in range(KT):
                    mm = pe.matmul(banks[:, h % 4, d * P:512], taps[:, r, h % GH, d * P:(d + 1) * P],
                                   xin[:, r, 0:KT - d, (h % GH) * B:(h % GH + 1) * B], start=(d == 0), stop=(d == KT - 1))
                m = c_pe.by(mm)
                if h % GH == GH - 1:
                    used[g] = m
                    if g + NR < NG:
                        load_group(g + NR)
                wait(dve, m)
                evac[h] = c_dve.by(dve.tensor_tensor(y_t[:, :, h * B:(h + 1) * B],
                                                     banks[:, h % 4, :].rearrange("p (j b) -> p j b", j=KT), mask[:], ALU.mult))
            if h >= 1:
                c = h - 1
                wait(pe, evac[c])
                for j in range(KT):
                    mm = pe.matmul(banks[:, 7, c * E:(c + 1) * E], y_t[:, j, c * B:(c + 1) * B], gate_sb[:, j, :],
                                   start=(j == 0), stop=(j == KT - 1))
        m_gl = c_pe.by(mm)

        sc = sb("sc", [P, H, E])
        top = sb("top", [P, H, 8])
        idx = sb("idx", [P, H, 8], U32)
        idx_f = sb("idx_f", [P, H, TOPK])
        cw = sb("cw", [P, H, E])
        wt = sb("wt", [P, H, TOPK])
        ssum = sb("ssum", [P, H])
        hot = sb("hot", [P, H, E])
        wait(act, m_gl)
        m = c_act.by(act.activation(sc[:], banks[:, 7, :].rearrange("p (c e) -> p c e", c=H), ACT.Sigmoid))
        wait(dve, m)
        v(dve.tensor_tensor(sc[:], sc[:], bias_sb[:].unsqueeze(1).to_broadcast([P, H, E]), ALU.add))
        for c in range(H):
            mt = c_dve.by(dve.max(top[:, c, :], sc[:, c, :]))
        wait(dve, mt)
        for c in range(H):
            mt = c_dve.by(dve.max_index(idx[:, c, :], top[:, c, :], sc[:, c, :]))
        wait(dve, mt)
        v(dve.tensor_copy(idx_f[:], idx[:, :, 0:TOPK]))
        v(dve.tensor_reduce(ssum[:], top[:, :, 0:TOPK], mybir.AxisListType.X, ALU.add))
        v(dve.tensor_scalar(ssum[:], ssum[:], 1e-20, None, ALU.add))
        v(dve.reciprocal(ssum[:], ssum[:]))
        v(dve.tensor_tensor(wt[:], top[:, :, 0:TOPK], ssum[:].unsqueeze(2).to_broadcast([P, H, TOPK]), ALU.mult))
        full = [P, H, E]
        for k in range(TOPK):
            v(dve.tensor_tensor(hot[:], iota_e[:].unsqueeze(1).to_broadcast(full), idx_f[:, :, k:k + 1].to_broadcast(full), ALU.is_equal))
            if k == 0:
                v(dve.tensor_tensor(cw[:], hot[:], wt[:, :, k:k + 1].to_broadcast(full), ALU.mult))
            else:
                v(dve.tensor_tensor(hot[:], hot[:], wt[:, :, k:k + 1].to_broadcast(full), ALU.mult))
                m_cw = v(dve.tensor_tensor(cw[:], cw[:], hot[:], ALU.add))

        acc = arena[:].rearrange("p (c n) -> p c n", c=H)
        c_x = count("c_x")
        wait(nc.sync, m_k)
        m_x = c_x.by(nc.sync.dma_start(acc, x), 16)
        w_up = sb("w_up", [P, 2, KT, 2, I])
        w_dn = taps[:, :, 0:IT, :]
        wait(nc.sync, used[NG - 1])
        c_w = [count("c_w0"), count("c_w1")]
        act_sb = xin[:, 0].rearrange("p (s i) t -> p s i t", s=2)
        z = xin[:, 1].rearrange("p (s i) t -> p s i t", s=2)
        w_used, w_in = {}, {}

        def load_expert(e):
            r = e % 2
            if e >= 2:
                wait(nc.sync, w_used[e - 2])
            g_, u_, d_ = (wg[e], wu[e], wd[e]) if e < E else (sg, su, sd)
            c_w[r].by(nc.sync.dma_start(w_up[:, r, :, 0, :], g_), 16)
            c_w[r].by(nc.sync.dma_start(w_up[:, r, :, 1, :], u_), 16)
            w_in[e] = c_w[r].by(nc.sync.dma_start(w_dn[:, r], d_), 16)

        load_expert(0)
        load_expert(1)
        steps = [(e, g) for e in range(E + 1) for g in range(NG)]
        up_free, z_ready, z_free, dn_free = {}, {}, {}, {}
        wait(dve, m_x)
        nd = 0
        for s in range(len(steps) + 1):
            if s < len(steps):
                e, g = steps[s]
                r = e % 2
                if g == 0:
                    wait(pe, w_in[e])
                for i in range(IT):
                    if s >= 1:
                        wait(pe, up_free[s - 1, i])
                    for k2 in range(2):
                        for j in range(KT):
                            mm = pe.matmul(banks[:, 2 * i + k2, :], w_up[:, r, j, k2, i * P:(i + 1) * P],
                                           y_t[:, j, g * 512:(g + 1) * 512], start=(j == 0), stop=(j == KT - 1))
                    m = c_pe.by(mm)
                    wait(act, m)
                    if s >= 2:
                        wait(act, z_ready[s - 2, i])
                    ma = c_act.by(act.activation(act_sb[:, s % 2, i, :], banks[:, 2 * i, :], ACT.Silu))
                    wait(dve, ma)
                    if s >= 2:
                        wait(dve, z_free[s - 2])
                    z_ready[s, i] = up_free[s, i] = c_dve.by(dve.tensor_tensor(z[:, s % 2, i, :], act_sb[:, s % 2, i, :], banks[:, 2 * i + 1, :], ALU.mult))
            if s >= 1:
                q = s - 1
                e, g = steps[q]
                r = e % 2
                wait(pe, z_ready[q, IT - 1])
                for t in range(GH):
                    bank = 4 + nd % 4
                    if nd >= 4:
                        wait(pe, dn_free[nd - 4])
                    for i in range(IT):
                        mm = pe.matmul(banks[:, bank, :], z[:, q % 2, i, t * P:(t + 1) * P], w_dn[:, r, i, :], start=(i == 0), stop=(i == IT - 1))
                    m = c_pe.by(mm)
                    c = g * GH + t
                    wait(dve, m)
                    if e < E:
                        ins = dve.scalar_tensor_tensor(out=acc[:, c, :], in0=banks[:, bank, :], scalar=cw[:, c, e:e + 1], in1=acc[:, c, :], op0=ALU.mult, op1=ALU.add)
                    else:
                        ins = dve.tensor_tensor(acc[:, c, :], banks[:, bank, :], acc[:, c, :], ALU.add)
                    dn_free[nd] = c_dve.by(ins)
                    nd += 1
                z_free[q] = m
                if g == NG - 1:
                    w_used[e] = m
                    if e + 2 <= E:
                        load_expert(e + 2)
        c_out = count("c_out")
        wait(nc.sync, dn_free[nd - 1])
        m_out = c_out.by(nc.sync.dma_start(out, acc), 16)
        wait(nc.sync, m_out)


def kernel(x, itok_B_78_3631, L0_cond_log_dt, L0_cond_C, L0_cond_log_A_real, L0_cond_A_imag, L0_cond_D,
           L0_ffn_gate_w, L0_ffn_bias, L0_ffn_Wg, L0_ffn_Wu, L0_ffn_Wd, L0_ffn_Sg, L0_ffn_Su, L0_ffn_Sd):
    import numpy as np
    import concourse.bacc as bacc
    from concourse.bass_utils import run_bass_kernel_spmd

    def a(v):
        return np.asarray(v)

    def k_major(w, rows):
        w = np.swapaxes(a(w), -1, -2)
        w = w.reshape(*w.shape[:-2], rows // P, P, w.shape[-1])
        return np.ascontiguousarray(np.swapaxes(w, -3, -2))

    xn = a(x)
    arrays = {
        "x": np.ascontiguousarray(xn),
        "xT": np.ascontiguousarray(xn.transpose(2, 1, 0).reshape(KT, P, H * B)[:, ::-1]),
        "lens": a(itok_B_78_3631).reshape(1, B),
        "log_dt": a(L0_cond_log_dt).reshape(1, H),
        "c_re": np.ascontiguousarray(a(L0_cond_C)[..., 0].T),
        "c_im": np.ascontiguousarray(a(L0_cond_C)[..., 1].T),
        "log_a": np.ascontiguousarray(a(L0_cond_log_A_real).T),
        "a_im": np.ascontiguousarray(a(L0_cond_A_imag).T),
        "d_skip": a(L0_cond_D).reshape(1, H),
        "gate_w": k_major(L0_ffn_gate_w, L),
        "bias": a(L0_ffn_bias).reshape(1, E),
        "wg": k_major(L0_ffn_Wg, L), "wu": k_major(L0_ffn_Wu, L), "wd": k_major(L0_ffn_Wd, I),
        "sg": k_major(L0_ffn_Sg, L), "su": k_major(L0_ffn_Su, L), "sd": k_major(L0_ffn_Sd, I),
    }
    nc = bacc.Bacc("TRN2", target_bir_lowering=False, num_devices=1)
    args = {}
    for name, arr in arrays.items():
        args[name] = nc.dram_tensor(name, arr.shape, mybir.dt.from_np(arr.dtype), kind="ExternalInput").ap()
    args["out"] = nc.dram_tensor("out", (B, H, L), F32, kind="ExternalOutput").ap()
    args["kpad"] = nc.dram_tensor("kpad", (H, KPITCH), F32).ap()
    build(nc, **args)
    r = run_bass_kernel_spmd(nc, [arrays], core_ids=[0])
    return r.results[0]["out"]
```

```python
from contextlib import ExitStack

import concourse.bass as bass
from concourse import mybir

P = 128
F32 = mybir.dt.float32
I32 = mybir.dt.int32
U32 = mybir.dt.uint32
F32R = mybir.dt.float32r
ALU = mybir.AluOpType
ACT = mybir.ActivationFunctionType

B, H, L = 128, 32, 512
N = 64
E, I, TOPK = 16, 256, 4
KT = L // P
IT = I // P
VLEN, ULEN = 32, 16
SLOTS = B * H * TOPK
NT = (SLOTS + E * (P - 1)) // P
NW = 4
S0 = 18
KPITCH = 640
GH = 4
NG = H // GH

TWO_PI = 6.283185307179586
C1, C2 = 6.28125, 0.00193500518798828125
C3 = TWO_PI - C1 - C2
LN2_HI, LN2_LO = 0.693359375, -2.12194440054690583e-4
ROUND = 12582912.0


class Count:

    def __init__(self, sem):
        self.sem, self.n = sem, 0

    def by(self, instruction, k=1):
        instruction.then_inc(self.sem, k)
        self.n += k
        return self.sem, self.n


def wait(engine, *marks):
    for sem, n in marks:
        engine.wait_ge(sem, n)


def build(nc, x, xT, lens, log_dt, c_re, c_im, log_a, a_im, d_skip, gate_w, bias, w_all, out, kpad, yrow, accs):
    with ExitStack() as ctx:
        def sb(name, shape, dt=F32):
            return ctx.enter_context(nc.sbuf_tensor(name, shape, dt))

        def count(name):
            return Count(ctx.enter_context(nc.semaphore(name)))

        banks = ctx.enter_context(nc.psum_tensor("banks", [P, 8, 512], F32))
        TABLES = H * 4 * (VLEN + 2 * ULEN + 2)
        GROUP = KT * GH * B
        area = sb("area", [P, TABLES + 2 * GROUP])
        arena = area[:, 0:TABLES]
        pe, act, dve, pool = nc.tensor, nc.scalar, nc.vector, nc.gpsimd
        c_pe, c_act, c_dve, c_pool = count("c_pe"), count("c_act"), count("c_dve"), count("c_pool")

        def v(ins):
            m = c_dve.by(ins)
            wait(dve, m)
            return m

        par = sb("par", [P, 6, H])
        d_row = sb("d_row", [1, H])
        len_i = sb("len_i", [P, 1], I32)
        row_int = sb("row_int", [P, L], I32)
        part_i = sb("part_i", [P, 1], I32)
        gate_sb = sb("gate_sb", [P, KT, E])
        bias_sb = sb("bias_sb", [P, E])
        zero = sb("zero", [P, P])
        c_par, c_gate = count("c_par"), count("c_gate")
        nc.sync.dma_start(par[:, 0, :], log_dt.partition_broadcast(P)).then_inc(c_par.sem, 16)
        for half in range(2):
            q = slice(N * half, N * half + N)
            for j, src in ((1, log_a), (2, a_im), (3, c_re), (4, c_im)):
                nc.sync.dma_start(par[q, j, :], src).then_inc(c_par.sem, 16)
        c_par.n = 16 * 9
        m_par = (c_par.sem, c_par.n)
        m_d = c_gate.by(nc.scalar.dma_start(d_row[:], d_skip), 16)
        c_gate.by(nc.scalar.dma_start(len_i[:], lens), 16)
        c_gate.by(nc.scalar.dma_start(gate_sb[:], gate_w), 16)
        m_gate = c_gate.by(nc.scalar.dma_start(bias_sb[:], bias.partition_broadcast(P)), 16)

        NJ = VLEN + 2 * ULEN + 2
        X0, Y0, S1, SH = VLEN, VLEN + ULEN, NJ - 2, NJ - 1
        l_tab = sb("l_tab", [P, NJ])
        q_tab = sb("q_tab", [P, NJ])
        c_pool.by(pool.iota(l_tab[:, 0:VLEN], [[1, VLEN]], base=0, channel_multiplier=0, allow_small_or_imprecise_dtypes=True))
        c_pool.by(pool.iota(l_tab[:, X0:S1].rearrange("p (k a) -> p k a", k=2), [[0, 2], [VLEN, ULEN]], base=0,
                            channel_multiplier=0, allow_small_or_imprecise_dtypes=True))
        m_iota = (c_pool.sem, c_pool.n)
        c_pool.by(pool.iota(part_i[:], [[0, 1]], base=0, channel_multiplier=1))
        m_row = c_pool.by(pool.iota(row_int[:], [[1, L]], base=0, channel_multiplier=0))
        dve.memset(l_tab[:, S1:SH], 1.0)
        dve.memset(l_tab[:, SH:NJ], 0.5)
        for lo, quarters in ((0, (1, 1, 2)), (N, (0, 2, 3))):
            q = slice(lo, lo + N)
            dve.memset(q_tab[q, 0:X0], quarters[0] / 4)
            dve.memset(q_tab[q, X0:Y0], quarters[1] / 4)
            dve.memset(q_tab[q, Y0:S1], quarters[2] / 4)
        dve.memset(q_tab[:, S1:NJ], 0.0)
        m_zero = v(dve.memset(zero[:], 0.0))

        area2 = sb("area2", [P, 24 * 2 * H + H * VLEN])
        sm = area2[:, 0:24 * 2 * H].rearrange("p (j w) -> p j w", j=24)
        sm_i = sb("sm_i", [P, 2 * H], I32)

        def accurate_exp(dst, dst_m1, src, w):
            t, k, r, q, s = (sm[:, 16 + j, 0:w] for j in range(5))
            v(dve.tensor_scalar(t, src, -87.0, 88.0, ALU.max, ALU.min))
            v(dve.tensor_scalar(k, t, 1.4426950408889634, ROUND, ALU.mult, ALU.add))
            v(dve.tensor_scalar(k, k, ROUND, None, ALU.subtract))
            v(dve.scalar_tensor_tensor(out=r, in0=k, scalar=-LN2_HI, in1=t, op0=ALU.mult, op1=ALU.add))
            v(dve.scalar_tensor_tensor(out=r, in0=k, scalar=-LN2_LO, in1=r, op0=ALU.mult, op1=ALU.add))
            v(dve.tensor_scalar(q, r, 1 / 5040, None, ALU.mult))
            for c in (1 / 720, 1 / 120, 1 / 24, 1 / 6, 0.5, 1.0):
                v(dve.scalar_tensor_tensor(out=q, in0=q, scalar=c, in1=r, op0=ALU.add, op1=ALU.mult))
            v(dve.tensor_scalar(sm_i[:, 0:w], k, 127.0, 8388608.0, ALU.add, ALU.mult))
            two_k = sm_i[:, 0:w].bitcast(F32)
            v(dve.tensor_tensor(q, q, two_k, ALU.mult))
            if dst_m1 is not None:
                v(dve.tensor_scalar(s, two_k, -1.0, None, ALU.add))
                v(dve.tensor_tensor(dst_m1, q, s, ALU.add))
            return v(dve.tensor_tensor(dst, q, two_k, ALU.add))

        wait(dve, m_par)
        exps = sm[:, 0, :]
        accurate_exp(exps, None, par[:, 0:2, :].rearrange("p a h -> p (a h)"), 2 * H)
        dt, neg_are = sm[:, 0, 0:H], sm[:, 0, H:2 * H]
        aim = par[:, 2, :]
        are, d_re, d_im = sm[:, 1, 0:H], sm[:, 2, 0:H], sm[:, 3, 0:H]
        v(dve.tensor_scalar(are, neg_are, -1.0, None, ALU.mult))
        v(dve.tensor_tensor(d_re, are, dt, ALU.mult))
        v(dve.tensor_tensor(d_im, aim, dt, ALU.mult))

        NM = VLEN + ULEN
        ang = arena[:, 0:H * NJ].rearrange("p (h j) -> p h j", h=H)
        turns = arena[:, H * NJ:2 * H * NJ].rearrange("p (h j) -> p h j", h=H)
        sin = arena[:, 2 * H * NJ:3 * H * NJ].rearrange("p (h j) -> p h j", h=H)
        mag = arena[:, 3 * H * NJ:3 * H * NJ + H * NM].rearrange("p (h j) -> p h j", h=H)
        wide = [P, H, NJ]
        wait(dve, m_iota)
        m_mag = v(dve.tensor_tensor(mag, d_re.unsqueeze(2).to_broadcast([P, H, NM]),
                                    l_tab[:, 0:NM].unsqueeze(1).to_broadcast([P, H, NM]), ALU.mult))
        wait(act, m_mag)
        m_mag = c_act.by(act.activation(mag, mag, ACT.Exp))
        v(dve.tensor_tensor(ang, d_im.unsqueeze(2).to_broadcast(wide), l_tab[:].unsqueeze(1).to_broadcast(wide), ALU.mult))
        q_wide = q_tab[:].unsqueeze(1).to_broadcast(wide)
        v(dve.scalar_tensor_tensor(out=turns, in0=ang, scalar=1 / TWO_PI, in1=q_wide, op0=ALU.mult, op1=ALU.add))
        v(dve.tensor_scalar(turns, turns, ROUND, ROUND, ALU.add, ALU.subtract))
        for part in (C1, C2, C3):
            v(dve.scalar_tensor_tensor(out=ang, in0=turns, scalar=-part, in1=ang, op0=ALU.mult, op1=ALU.add))
        v(dve.scalar_tensor_tensor(out=ang, in0=q_wide, scalar=TWO_PI, in1=ang, op0=ALU.mult, op1=ALU.add))
        m_ang = v(dve.tensor_scalar(ang, ang, 3.1415925, -3.1415925, ALU.min, ALU.max))
        wait(act, m_ang)
        m_sin = c_act.by(act.activation(sin, ang, ACT.Sin))

        ew, em = sm[:, 4, 0:H], sm[:, 5, 0:H]
        accurate_exp(ew, em, d_re, H)
        t0, t1, nr, ni, rd, gr, gi, ctr, cti = (sm[:, 6 + j, 0:H] for j in range(9))
        v(dve.tensor_tensor(t0, are, are, ALU.mult))
        v(dve.tensor_tensor(t1, aim, aim, ALU.mult))
        v(dve.tensor_tensor(t0, t0, t1, ALU.add))
        v(dve.tensor_scalar(t0, t0, 0.5, None, ALU.mult))
        v(dve.reciprocal(rd, t0))
        wait(dve, m_sin)
        s_one, s_half = sin[:, :, S1], sin[:, :, SH]
        v(dve.scalar_tensor_tensor(out=t0, in0=s_half, scalar=2.0, in1=s_half, op0=ALU.mult, op1=ALU.mult))
        v(dve.tensor_tensor(t0, t0, ew, ALU.mult))
        v(dve.tensor_tensor(nr, em, t0, ALU.subtract))
        v(dve.tensor_tensor(ni, ew, s_one, ALU.mult))
        for dst, a, b_, op in ((gr, (nr, are), (ni, aim), ALU.add), (gi, (ni, are), (nr, aim), ALU.subtract)):
            v(dve.tensor_tensor(t0, *a, ALU.mult))
            v(dve.tensor_tensor(t1, *b_, ALU.mult))
            v(dve.tensor_tensor(t0, t0, t1, op))
            v(dve.tensor_tensor(dst, t0, rd, ALU.mult))
        cre, cim = par[:, 3, :], par[:, 4, :]
        for dst, a, b_, op in ((ctr, (cre, gr), (cim, gi), ALU.subtract), (cti, (cre, gi), (cim, gr), ALU.add)):
            v(dve.tensor_tensor(t0, *a, ALU.mult))
            v(dve.tensor_tensor(t1, *b_, ALU.mult))
            v(dve.tensor_tensor(dst, t0, t1, op))
        u_wide = [P, H, ULEN]
        u_x, u_y = sin[:, :, X0:Y0], sin[:, :, Y0:S1]
        v(dve.tensor_tensor(u_x, u_x, ctr.unsqueeze(2).to_broadcast(u_wide), ALU.mult))
        v(dve.tensor_tensor(u_y, u_y, cti.unsqueeze(2).to_broadcast(u_wide), ALU.mult))
        v(dve.tensor_tensor(u_x, u_x, u_y, ALU.add))
        wait(dve, m_mag)
        v(dve.tensor_tensor(u_x, u_x, mag[:, :, VLEN:NM], ALU.mult))
        m_uv = v(dve.tensor_tensor(sin[:, :, 0:VLEN], sin[:, :, 0:VLEN], mag[:, :, 0:VLEN], ALU.mult))

        wait(pe, m_uv)
        for h in range(H):
            k_ps = banks[0:ULEN, 4 + h // 16, (h % 16) * VLEN:(h % 16 + 1) * VLEN]
            mm = pe.matmul(k_ps, u_x[:, h, :], sin[:, h, 0:VLEN], start=True, stop=True)
        m_k = c_pe.by(mm)
        k_sb = area2[0:ULEN, 24 * 2 * H:].rearrange("a (h b) -> a h b", h=H)
        wait(dve, m_k)
        v(dve.tensor_copy(k_sb.rearrange("a (g h) b -> a g (h b)", g=2), banks[0:ULEN, 4:6, :]))
        wait(dve, m_gate)
        m_ksb = v(dve.tensor_tensor(k_sb[0:1, :, 0], k_sb[0:1, :, 0], d_row[:], ALU.add))
        c_kpad = count("c_kpad")
        kh = kpad.tensor
        wait(nc.sync, m_zero)
        c_kpad.by(nc.sync.dma_start(bass.AP(kh, 0, [[KPITCH, H], [1, P - 1]]), zero[0:H, 0:P - 1]), 16)
        wait(nc.sync, m_ksb)
        m_kpad = c_kpad.by(nc.sync.dma_start(bass.AP(kh, P - 1, [[VLEN, ULEN], [KPITCH, H], [1, VLEN]]), k_sb), 16)

        ident = sb("ident", [P, P])
        row_i = sb("row_i", [P, L])
        part_f = sb("part_f", [P, 1])
        len_f = sb("len_f", [P, 1])
        wait(dve, m_row)
        v(dve.tensor_copy(row_i[:], row_int[:]))
        v(dve.tensor_copy(part_f[:], part_i[:]))
        v(dve.tensor_copy(len_f[:], len_i[:]))
        m_ident = v(dve.tensor_scalar(ident[:], row_i[:, 0:P], part_f[:, 0:1], None, ALU.is_equal))

        NR = 2
        taps = area[:, 0:NR * GROUP].rearrange("p (r h c) -> p r h c", r=NR, h=GH)
        xin = area[:, TABLES:].rearrange("p (r k t) -> p r k t", r=NR, k=KT)
        y_row = sb("y_row", [P, 3, L])
        y_tr = sb("y_tr", [P, 2, L])
        c_taps = [count(f"c_taps{i}") for i in range(NR)]
        c_xin = [count(f"c_xin{i}") for i in range(NR)]
        c_yst = [count(f"c_yst{i}") for i in range(3)]
        loaded, used, rows, stored, turned, evac = {}, {}, {}, {}, {}, {}

        def load_inputs(g):
            r = g % NR
            if g >= NR:
                wait(nc.sync, used[g - NR])
            m = c_xin[r].by(nc.sync.dma_start(xin[:, r], xT[:, :, g * GH * B:(g + 1) * GH * B].rearrange("m p t -> p m t")), 16)
            if g == 0:
                wait(nc.sync, m_kpad)
            loaded[g] = (m, c_taps[r].by(nc.sync.dma_start(
                taps[:, r], bass.AP(kh, KPITCH * GH * g, [[1, P], [KPITCH, GH], [1, 512]])), 16))

        for g in range(NR):
            load_inputs(g)
        wait(pe, m_gate, m_ident)
        for h in range(H + 2):
            if h < H:
                g, r = h // GH, (h // GH) % NR
                if h % GH == 0:
                    wait(pe, *loaded[g])
                if h >= 3:
                    wait(pe, rows[h - 3])
                for m_ in range(KT):
                    mm = pe.matmul(banks[:, h % 3, m_ * P:512], xin[:, r, m_, (h % GH) * B:(h % GH + 1) * B],
                                   taps[:, r, h % GH, 0:512 - m_ * P], start=(m_ == 0), stop=(m_ == KT - 1))
                m = c_pe.by(mm)
                if h % GH == GH - 1:
                    used[g] = m
                    if g + NR < NG:
                        load_inputs(g + NR)
                wait(dve, m)
                if h >= 3:
                    wait(dve, stored[h - 3], turned[h - 3])
                rows[h] = c_dve.by(dve.scalar_tensor_tensor(
                    out=y_row[:, h % 3, :], in0=row_i[:], scalar=len_f[:, 0:1], in1=banks[:, h % 3, :], op0=ALU.is_lt, op1=ALU.mult))
                wait(nc.scalar, rows[h])
                stored[h] = c_yst[h % 3].by(nc.scalar.dma_start(yrow[h * B:(h + 1) * B, 0:L], y_row[:, h % 3, :]), 16)
            if 1 <= h <= H:
                c = h - 1
                wait(pe, rows[c])
                if c >= 2:
                    wait(pe, evac[c - 2])
                for j in range(KT):
                    mm = pe.transpose(banks[:, 3 + c % 2, j * P:(j + 1) * P], y_row[:, c % 3, j * P:(j + 1) * P], ident[:])
                turned[c] = c_pe.by(mm)
                wait(act, turned[c])
                evac[c] = c_act.by(act.copy(y_tr[:, c % 2, :], banks[:, 3 + c % 2, :]))
            if h >= 2:
                c = h - 2
                wait(pe, evac[c])
                for j in range(KT):
                    mm = pe.matmul(banks[:, 7, c * E:(c + 1) * E], y_tr[:, c % 2, j * P:(j + 1) * P], gate_sb[:, j, :],
                                   start=(j == 0), stop=(j == KT - 1))
                m_gl = c_pe.by(mm)

        F16 = mybir.dt.float16
        sc = sb("sc", [P, H, E])
        top = sb("top", [P, H, 8])
        idx = sb("idx", [P, H, 8], U32)
        idx_f = sb("idx_f", [P, H, TOPK])
        cw = y_tr[:, 0, :].rearrange("p (c e) -> p c e", c=H)
        wt = sb("wt", [P, H, TOPK])
        ssum = sb("ssum", [P, H])
        hot = area2[:, 0:TOPK * H * E].rearrange("p (k c e) -> p k c e", k=TOPK, c=H)
        tmp = sc
        picked = sb("picked", [P, H, E], F16)
        ones16 = sb("ones16", [P, P], F16)
        before16 = sb("before16", [P, P], F16)
        v(dve.memset(ones16[:], 1.0))
        v(dve.tensor_scalar(before16[:], row_i[:, 0:P], part_f[:, 0:1], None, ALU.is_gt))
        full = [P, H, E]
        wait(act, m_gl)
        m = c_act.by(act.activation(sc[:], banks[:, 7, :].rearrange("p (c e) -> p c e", c=H), ACT.Sigmoid))
        wait(dve, m)
        v(dve.tensor_tensor(sc[:], sc[:], bias_sb[:].unsqueeze(1).to_broadcast(full), ALU.add))
        for c in range(H):
            m = c_dve.by(dve.max(top[:, c, :], sc[:, c, :]))
        wait(dve, m)
        for c in range(H):
            m = c_dve.by(dve.max_index(idx[:, c, :], top[:, c, :], sc[:, c, :]))
        wait(dve, m)
        v(dve.tensor_copy(idx_f[:], idx[:, :, 0:TOPK]))
        for k in range(TOPK):
            v(dve.tensor_tensor(hot[:, k], row_i[:, 0:E].unsqueeze(1).to_broadcast(full), idx_f[:, :, k:k + 1].to_broadcast(full), ALU.is_equal))
        v(dve.tensor_tensor(tmp[:], hot[:, 0], hot[:, 1], ALU.add))
        v(dve.tensor_tensor(tmp[:], tmp[:], hot[:, 2], ALU.add))
        m_picked = v(dve.tensor_tensor(picked[:], tmp[:], hot[:, 3], ALU.add))

        wait(pe, m_picked)
        mm = pe.matmul(banks[:, 5, :], before16[:], picked[:].rearrange("p c e -> p (c e)"), start=True, stop=False)
        for c in range(H - 1):
            mm = pe.matmul(banks[:, 5, (c + 1) * E:512], ones16[:], picked[:, c:c + 1, :].to_broadcast([P, H - 1 - c, E]),
                           start=False, stop=(c == H - 2))
        for c in range(H):
            mm = pe.matmul(banks[:, 6, 0:E], ones16[:], picked[:, c, :], start=(c == 0), stop=(c == H - 1))
        m_rank = c_pe.by(mm)

        v(dve.tensor_reduce(ssum[:], top[:, :, 0:TOPK], mybir.AxisListType.X, ALU.add))
        v(dve.tensor_scalar(ssum[:], ssum[:], 1e-20, None, ALU.add))
        v(dve.reciprocal(ssum[:], ssum[:]))
        v(dve.tensor_tensor(wt[:], top[:, :, 0:TOPK], ssum[:].unsqueeze(2).to_broadcast([P, H, TOPK]), ALU.mult))
        v(dve.tensor_tensor(cw[:], hot[:, 0], wt[:, :, 0:1].to_broadcast(full), ALU.mult))
        for k in range(1, TOPK):
            v(dve.tensor_tensor(tmp[:], hot[:, k], wt[:, :, k:k + 1].to_broadcast(full), ALU.mult))
            m_cw = v(dve.tensor_tensor(cw[:], cw[:], tmp[:], ALU.add))
        c_cw = count("c_cw")
        wait(nc.sync, m_cw)
        m_cwst = c_cw.by(nc.sync.dma_start(yrow[:, L:L + E].rearrange("(c p) e -> p c e", p=P), cw[:]), 16)

        cum = sb("cum", [P, 2, 2 * E])
        rank = y_tr[:, 1, :].rearrange("p (c e) -> p c e", c=H)
        slot = sb("slot", [P, H, TOPK])
        slot_a = sb("slot_a", [P, H, TOPK])
        slot_b = sb("slot_b", [P, H, TOPK])
        wait(dve, m_rank)
        v(dve.memset(cum[:], 0.0))
        v(dve.tensor_scalar(cum[:, 0, E:], banks[:, 6, 0:E], P / 2 - 0.5, 1 / P, ALU.add, ALU.mult))
        v(dve.tensor_scalar(cum[:, 0, E:], cum[:, 0, E:], ROUND, ROUND, ALU.add, ALU.subtract))
        for n, d in enumerate((1, 2, 4, 8)):
            v(dve.tensor_tensor(cum[:, (n + 1) % 2, E:], cum[:, n % 2, E:], cum[:, n % 2, E - d:2 * E - d], ALU.add))
        cum_incl, cum_excl = cum[:, 0, E:2 * E], cum[:, 0, E - 1:2 * E - 1]
        v(dve.scalar_tensor_tensor(out=rank[:], in0=cum_excl.unsqueeze(1).to_broadcast(full), scalar=float(P),
                                   in1=banks[:, 5, :].rearrange("p (c e) -> p c e", c=H), op0=ALU.mult, op1=ALU.add))
        for k in range(TOPK):
            v(dve.tensor_tensor(tmp[:], hot[:, k], rank[:], ALU.mult))
            v(dve.tensor_reduce(slot[:, :, k], tmp[:], mybir.AxisListType.X, ALU.add))
        v(dve.tensor_scalar(slot_a[:], slot[:], -(P / 2 - 0.5), 1 / P, ALU.add, ALU.mult))
        v(dve.tensor_scalar(slot_a[:], slot_a[:], ROUND, ROUND, ALU.add, ALU.subtract))
        v(dve.scalar_tensor_tensor(out=slot_b[:], in0=slot_a[:], scalar=-float(P), in1=slot[:], op0=ALU.mult, op1=ALU.add))

        tile_e = sb("tile_e", [P, NT])
        tile_hot = sb("tile_hot", [P, NT, E], F16)
        meta = sb("meta", [1, 2, NT], I32)
        changed = sb("changed", [1, NT])
        wide_t = [P, NT, E]
        v(dve.tensor_tensor(tile_hot[:], row_i[:, 0:NT].unsqueeze(2).to_broadcast(wide_t), cum_incl.unsqueeze(1).to_broadcast(wide_t), ALU.is_ge))
        v(dve.tensor_reduce(tile_e[:], tile_hot[:], mybir.AxisListType.X, ALU.add))
        v(dve.tensor_scalar(tile_e[:], tile_e[:], float(E - 1), None, ALU.min))
        v(dve.tensor_copy(meta[:, 0, :], tile_e[0:1, :]))
        v(dve.memset(changed[:], 1.0))
        v(dve.tensor_tensor(changed[:, NW:], tile_e[0:1, NW:], tile_e[0:1, 0:NT - NW], ALU.not_equal))
        m_meta = v(dve.tensor_copy(meta[:, 1, :], changed[:]))
        v(dve.tensor_tensor(tile_hot[:], tile_e[:].unsqueeze(2).to_broadcast(wide_t), row_i[:, 0:E].unsqueeze(1).to_broadcast(wide_t), ALU.is_equal))

        row16 = sb("row16", [P, NT + 1], F16)
        token1 = sb("token1", [P, H])
        NB = 4
        b_hot = sb("b_hot", [P, NB, P], F16)
        a_tok = sb("a_tok", [P, NB, NT], F16)
        v(dve.tensor_copy(row16[:], row_i[:, 0:NT + 1]))
        v(dve.tensor_scalar(token1[:], row_i[:, 0:H], float(P), 1.0, ALU.mult, ALU.add))
        v(dve.tensor_scalar(token1[:, H // 2:], token1[:, H // 2:], -2048.0, None, ALU.add))
        v(dve.tensor_scalar(token1[:], token1[:], part_f[:, 0:1], None, ALU.add))
        freed = {}
        for n in range(H * TOPK):
            c, k, r = n // TOPK, n % TOPK, n % NB
            if n >= NB:
                wait(dve, freed[n - NB])
            c_dve.by(dve.tensor_scalar(b_hot[:, r], row16[:, 0:P], slot_b[:, c, k:k + 1], None, ALU.is_equal))
            m = c_dve.by(dve.tensor_scalar(a_tok[:, r], row16[:, 0:NT], slot_a[:, c, k:k + 1], token1[:, c:c + 1], ALU.is_equal, ALU.mult))
            wait(pe, m)
            half = c // (H // 2)
            mm = pe.matmul(banks[:, 5 + half, 0:NT], b_hot[:, r], a_tok[:, r], start=(n % (H * TOPK // 2) == 0),
                           stop=(n % (H * TOPK // 2) == H * TOPK // 2 - 1))
            freed[n] = c_pe.by(mm)
        g_idx = sb("g_idx", [P, NT], I32)
        s_idx = sb("s_idx", [P, NT], I32)
        tok = sb("tok", [P, NT])
        upper = sb("upper", [P, NT])
        wait(dve, freed[H * TOPK - 1])
        v(dve.tensor_scalar(upper[:], banks[:, 6, 0:NT], 0.0, 2048.0, ALU.is_gt, ALU.mult))
        v(dve.tensor_tensor(upper[:], upper[:], banks[:, 6, 0:NT], ALU.add))
        v(dve.tensor_tensor(tok[:], upper[:], banks[:, 5, 0:NT], ALU.add))
        m_gidx = v(dve.tensor_scalar(g_idx[:], tok[:], -1.0, 0.0, ALU.add, ALU.max))
        v(dve.tensor_scalar(upper[:], tok[:], 0.0, float(H * B + 1), ALU.is_equal, ALU.mult))
        v(dve.tensor_tensor(tok[:], tok[:], upper[:], ALU.add))
        v(dve.tensor_scalar(upper[:], upper[:], 0.0, part_f[:, 0:1], ALU.is_gt, ALU.mult))
        m_sidx = v(dve.scalar_tensor_tensor(out=s_idx[:], in0=tok[:], scalar=-1.0, in1=upper[:], op0=ALU.add, op1=ALU.add))

        x_rows = x.rearrange("b h l -> h b l")
        out_rows = out.rearrange("b h l -> h b l")
        c_init, c_tail = count("c_init"), count("c_tail")
        acc_rows = accs[0:H * B, :].rearrange("(h b) l -> h b l", b=B)
        m_init = c_init.by(nc.sync.dma_start(acc_rows[S0:H], x_rows[S0:H]), 16)

        WF = 3 * 1024
        CH = 1024
        NRAW = 2
        at = [0]

        def part(*shape):
            n = 1
            for d in shape:
                n *= d
            at[0] += n
            names = "abc"[:len(shape)]
            return area[:, at[0] - n:at[0]].rearrange(f"p ({' '.join(names)}) -> p {' '.join(names)}", **dict(zip(names, shape)))

        wait(nc.sync, used[NG - 1])
        w_raw = part(NRAW, WF)
        w_hi = sb("w_hi", [P, NW, WF], F32R)
        w_lo = sb("w_lo", [P, NW, WF], F32R)
        rows_in = part(3, L + E)
        add_in = part(2, L)
        yt_hi = sb("yt_hi", [P, 2, KT, P], F32R)
        yt_lo = sb("yt_lo", [P, 2, KT, P], F32R)
        silu = part(2, I)
        z = part(2, I)
        zt_hi = sb("zt_hi", [P, 2, IT, P], F32R)
        zt_lo = sb("zt_lo", [P, 2, IT, P], F32R)
        o_sb = part(3, L)
        w_tok = sb("w_tok", [P, 4])
        junk = sb("junk", [P, E])
        c_raw = [count(f"c_raw{i}") for i in range(NRAW)]
        c_rg = [count(f"c_rg{i}") for i in range(3)]
        c_rl = [count(f"c_rl{i}") for i in range(3)]
        c_add = [count(f"c_add{i}") for i in range(2)]
        c_sa = [count(f"c_sa{i}") for i in range(3)]
        c_st = [count(f"c_st{i}") for i in range(3)]

        steps = [("first", c) for c in range(S0)] + [("expert", j) for j in range(NT)] + [("last", c) for c in range(S0, H)]
        NS = len(steps)
        in_ready, raw_ready, add_ready = {}, {}, {}
        hi_done, lo_done, ty, yh, yl, gu, si, zz, tz, zh, zl, dn, od, sent, wtk = ({} for _ in range(15))
        scattered = []

        def flag_of(s):
            kind, n = steps[s]
            first = 0 if kind == "first" else S0 if kind == "expert" else S0 + NT
            if s - first < NW:
                return True
            return n if kind == "expert" else False

        def fetch(s):
            kind, n = steps[s]
            r = s % 3
            if kind == "expert":
                if n == 0:
                    wait(pool, m_gidx, m_cwst, *[stored[c] for c in range(H - 3, H)])
                if s >= 3:
                    wait(pool, ty[s - 3])
                    if s - 3 in wtk:
                        wait(pool, wtk[s - 3])
                in_ready[s] = c_rg[r].by(pool.indirect_dma_start(
                    out=rows_in[:, r, :], out_offset=None, in_=yrow,
                    in_offset=bass.IndirectOffsetOnAxis(ap=g_idx[:, n:n + 1], axis=0)), 16)
            else:
                if s >= 3:
                    wait(nc.sync, ty[s - 3])
                    if s - 3 in wtk:
                        wait(nc.sync, wtk[s - 3])
                if s == 0:
                    wait(nc.sync, *[stored[c] for c in range(H - 3, H)])
                in_ready[s] = c_rl[r].by(nc.sync.dma_start(rows_in[:, r, 0:L], yrow[n * B:(n + 1) * B, 0:L]), 16)

        def fetch_addend(s):
            kind, n = steps[s]
            if kind == "expert":
                return
            if s - 2 in add_ready:
                wait(nc.sync, od[s - 2])
            if kind == "last" and n == S0:
                wait(nc.sync, scattered[-1])
                m_tail.append(c_tail.by(nc.sync.dma_start(out_rows[0:S0], acc_rows[0:S0]), 16))
            add_ready[s] = c_add[s % 2].by(nc.sync.dma_start(add_in[:, s % 2, :], x_rows[n] if kind == "first" else acc_rows[n]), 16)

        m_tail = []

        def fetch_weights(s):
            f = flag_of(s)
            if f is False:
                return
            kind, n = steps[s]
            q = s % NRAW
            for d in (hi_done, lo_done):
                last = [d[t] for t in raw_user[q] if t in d]
                wait(nc.sync, *last[-1:])
            if kind != "expert":
                raw_ready[s] = c_raw[q].by(nc.sync.dma_start(w_raw[:, q, :], w_all[E]), 16)
            else:
                if n == 0:
                    wait(nc.sync, m_meta)
                e = nc.sync.value_load(meta[0:1, 0, n:n + 1], min_val=0, max_val=E - 1)
                src = w_all[bass.ds(e, 1)].rearrange("o p n -> (o p) n")
                if f is True:
                    raw_ready[s] = c_raw[q].by(nc.sync.dma_start(w_raw[:, q, :], src), 16)
                else:
                    flag = nc.sync.value_load(meta[0:1, 1, n:n + 1], min_val=0, max_val=1)
                    raw_ready[s] = c_raw[q].by(nc.sync.dma_start(w_raw[:, q, :], src, cond=flag), 16)
            raw_user[q].append(s)

        raw_user = [[] for _ in range(NRAW)]

        def split_chunk(s, ch, flags):
            f = flag_of(s)
            if f is False or s >= NS:
                return
            q, r = s % NRAW, s % NW
            cs = slice(ch * CH, (ch + 1) * CH)
            if ch == 0:
                for eng in (act, dve):
                    wait(eng, raw_ready[s])
                    if s >= NW:
                        wait(eng, dn[s - NW])
            if f is True:
                m = c_act.by(act.copy(w_hi[:, r, cs], w_raw[:, q, cs]))
                wait(dve, m)
                ml = c_dve.by(dve.tensor_tensor(w_lo[:, r, cs], w_raw[:, q, cs], w_hi[:, r, cs].bitcast(F32), ALU.subtract))
            else:
                if ch == 0:
                    for name, eng in (("act", act), ("dve", dve)):
                        flags[name] = eng.value_load(meta[0:1, 1, f:f + 1], min_val=0, max_val=1)
                with act.If(flags["act"] == 1):
                    act.copy(w_hi[:, r, cs], w_raw[:, q, cs])
                m = c_act.by(act.drain())
                wait(dve, m)
                with dve.If(flags["dve"] == 1):
                    dve.tensor_tensor(w_lo[:, r, cs], w_raw[:, q, cs], w_hi[:, r, cs].bitcast(F32), ALU.subtract)
                ml = c_dve.by(dve.drain())
            hi_done[s], lo_done[s] = m, ml
            w_done[s, ch] = (m, ml)

        w_done = {}

        def turn_rows(s):
            kind, n = steps[s]
            r = s % 3
            wait(pe, in_ready[s])
            if s >= 2:
                wait(pe, yl[s - 2])
            for j in range(KT):
                mm = pe.transpose(banks[:, s % 2, j * P:(j + 1) * P], rows_in[:, r, j * P:(j + 1) * P], ident[:])
            ty[s] = c_pe.by(mm)

        def split_rows(s):
            kind, n = steps[s]
            wait(act, ty[s])
            if s >= 2:
                wait(act, gu[s - 2])
            hi, lo = (t[:, s % 2].rearrange("p j t -> p (j t)") for t in (yt_hi, yt_lo))
            yh[s] = c_act.by(act.copy(hi, banks[:, s % 2, :]))
            wait(dve, yh[s])
            yl[s] = c_dve.by(dve.tensor_tensor(lo, banks[:, s % 2, :], hi.bitcast(F32), ALU.subtract))
            if kind == "expert":
                wait(dve, in_ready[s])
                if s >= 4 and s - 4 in od:
                    wait(dve, od[s - 4])
                wtk[s] = c_dve.by(dve.tensor_tensor_reduce(junk[:], rows_in[:, s % 3, L:L + E], tile_hot[:, n, :], 1.0, 0.0,
                                                           ALU.mult, ALU.add, w_tok[:, s % 4:s % 4 + 1]))
                wait(dve, wtk[s])

        def up(s, half):
            r, b = s % NW, 2 + s % 2
            if half == 0:
                wait(pe, yh[s], yl[s])
                if s >= 2:
                    wait(pe, zz[s - 2])
            if (s, half) in w_done:
                wait(pe, *w_done[s, half])
            for j in (2 * half, 2 * half + 1):
                ws = slice(j * 512, (j + 1) * 512)
                for n, (yt, w) in enumerate(((yt_hi, w_hi), (yt_hi, w_lo), (yt_lo, w_hi))):
                    mm = pe.matmul(banks[:, b, :], yt[:, s % 2, j, :], w[:, r, ws], start=(j == 0 and n == 0),
                                   stop=(j == KT - 1 and n == 2))
            if half:
                gu[s] = c_pe.by(mm)

        def activate(s):
            b = 2 + s % 2
            wait(act, gu[s])
            if s >= 2:
                wait(act, zz[s - 2])
            si[s] = c_act.by(act.activation(silu[:, s % 2, :], banks[:, b, 0:I], ACT.Silu))
            wait(dve, si[s])
            if s >= 2:
                wait(dve, tz[s - 2])
            zz[s] = c_dve.by(dve.tensor_tensor(z[:, s % 2, :], silu[:, s % 2, :], banks[:, b, I:2 * I], ALU.mult))

        def turn_z(s):
            wait(pe, zz[s])
            if s >= 2:
                wait(pe, zl[s - 2])
            for j in range(IT):
                mm = pe.transpose(banks[:, 4 + s % 2, j * P:(j + 1) * P], z[:, s % 2, j * P:(j + 1) * P], ident[:])
            tz[s] = c_pe.by(mm)

        def split_z(s):
            wait(act, tz[s])
            if s >= 2:
                wait(act, dn[s - 2])
            hi, lo = (t[:, s % 2].rearrange("p j t -> p (j t)") for t in (zt_hi, zt_lo))
            zh[s] = c_act.by(act.copy(hi, banks[:, 4 + s % 2, 0:I]))
            wait(dve, zh[s])
            zl[s] = c_dve.by(dve.tensor_tensor(lo, banks[:, 4 + s % 2, 0:I], hi.bitcast(F32), ALU.subtract))

        def down(s):
            r, b = s % NW, 6 + s % 2
            wait(pe, zh[s], zl[s])
            if s >= 2:
                wait(pe, od[s - 2])
            if (s, 2) in w_done:
                wait(pe, *w_done[s, 2])
            for j in range(IT):
                ws = slice(2048 + j * 512, 2048 + (j + 1) * 512)
                for n, (zt, w) in enumerate(((zt_hi, w_hi), (zt_hi, w_lo), (zt_lo, w_hi))):
                    mm = pe.matmul(banks[:, b, :], zt[:, s % 2, j, :], w[:, r, ws], start=(j == 0 and n == 0),
                                   stop=(j == IT - 1 and n == 2))
            dn[s] = c_pe.by(mm)

        def finish(s):
            kind, n = steps[s]
            r, b = s % 3, 6 + s % 2
            eng = act if kind == "expert" else dve
            wait(eng, dn[s])
            if s >= 3:
                wait(eng, sent[s - 3])
            if kind == "expert":
                wait(act, wtk[s])
                od[s] = c_act.by(act.activation(o_sb[:, r, :], banks[:, b, :], ACT.Copy, scale=w_tok[:, s % 4:s % 4 + 1]))
                wait(pool, od[s])
                if n == 0:
                    wait(pool, m_init, m_sidx, *[sent[t] for t in range(S0 - 3, S0)])
                if scattered:
                    wait(pool, scattered[-1])
                sent[s] = c_sa[r].by(pool.indirect_dma_start(
                    out=accs, out_offset=bass.IndirectOffsetOnAxis(ap=s_idx[:, n:n + 1], axis=0),
                    in_=o_sb[:, r, :], in_offset=None, compute_op=ALU.add), 16)
                scattered.append(sent[s])
            else:
                wait(dve, add_ready[s])
                od[s] = c_dve.by(dve.tensor_tensor(o_sb[:, r, :], banks[:, b, :], add_in[:, s % 2, :], ALU.add))
                wait(nc.scalar, od[s])
                dst = acc_rows[n] if kind == "first" else out_rows[n]
                sent[s] = c_st[r].by(nc.scalar.dma_start(dst, o_sb[:, r, :]), 16)

        for s in range(2):
            fetch(s)
        for s in range(2):
            fetch_weights(s)
            for ch in range(3):
                split_chunk(s, ch, {})
        turn_rows(0)
        split_rows(0)
        for s in range(NS + 1):
            flags = {}
            if s + 2 < NS:
                fetch(s + 2)
                fetch_weights(s + 2)
            if s < NS:
                up(s, 0)
            if s >= 1:
                turn_z(s - 1)
            if s + 1 < NS:
                turn_rows(s + 1)
            if s >= 1:
                split_z(s - 1)
            if s + 2 < NS:
                split_chunk(s + 2, 0, flags)
            if s + 1 < NS:
                split_rows(s + 1)
            if s + 2 < NS:
                split_chunk(s + 2, 1, flags)
            if s < NS:
                up(s, 1)
                activate(s)
            if s >= 1:
                down(s - 1)
            if s + 2 < NS:
                split_chunk(s + 2, 2, flags)
            if s >= 1:
                finish(s - 1)
            if s < NS:
                fetch_addend(s)
        wait(nc.sync, m_tail[0], *[sent[s] for s in range(NS - 3, NS)])


def kernel(x, itok_B_78_3631, L0_cond_log_dt, L0_cond_C, L0_cond_log_A_real, L0_cond_A_imag, L0_cond_D,
           L0_ffn_gate_w, L0_ffn_bias, L0_ffn_Wg, L0_ffn_Wu, L0_ffn_Wd, L0_ffn_Sg, L0_ffn_Su, L0_ffn_Sd):
    import numpy as np
    import concourse.bacc as bacc
    from concourse.bass_utils import run_bass_kernel_spmd

    def a(v):
        return np.asarray(v)

    def k_major(w, rows):
        w = np.swapaxes(a(w), -1, -2)
        w = w.reshape(*w.shape[:-2], rows // P, P, w.shape[-1])
        return np.ascontiguousarray(np.swapaxes(w, -3, -2))

    def pack(wg, wu, wd):
        up = np.stack([k_major(wg, L), k_major(wu, L)], axis=-2)
        return np.concatenate([w.reshape(*w.shape[:w.ndim - k], -1) for w, k in ((up, 3), (k_major(wd, I), 2))], axis=-1)

    w_all = np.concatenate([pack(L0_ffn_Wg, L0_ffn_Wu, L0_ffn_Wd), pack(L0_ffn_Sg, L0_ffn_Su, L0_ffn_Sd)[None]])
    xn = a(x)
    arrays = {
        "x": np.ascontiguousarray(xn),
        "xT": np.ascontiguousarray(xn.transpose(2, 1, 0).reshape(KT, P, H * B)[:, ::-1]),
        "lens": a(itok_B_78_3631).reshape(B, 1),
        "log_dt": a(L0_cond_log_dt).reshape(1, H),
        "c_re": np.ascontiguousarray(a(L0_cond_C)[..., 0].T),
        "c_im": np.ascontiguousarray(a(L0_cond_C)[..., 1].T),
        "log_a": np.ascontiguousarray(a(L0_cond_log_A_real).T),
        "a_im": np.ascontiguousarray(a(L0_cond_A_imag).T),
        "d_skip": a(L0_cond_D).reshape(1, H),
        "gate_w": k_major(L0_ffn_gate_w, L),
        "bias": a(L0_ffn_bias).reshape(1, E),
        "w_all": w_all,
    }
    nc = bacc.Bacc("TRN2", target_bir_lowering=False, num_devices=1)
    args = {}
    for name, arr in arrays.items():
        args[name] = nc.dram_tensor(name, arr.shape, mybir.dt.from_np(arr.dtype), kind="ExternalInput").ap()
    args["out"] = nc.dram_tensor("out", (B, H, L), F32, kind="ExternalOutput").ap()
    args["kpad"] = nc.dram_tensor("kpad", (H, KPITCH), F32).ap()
    args["yrow"] = nc.dram_tensor("yrow", (H * B, L + E), F32).ap()
    args["accs"] = nc.dram_tensor("accs", (H * B + P, L), F32).ap()
    build(nc, **args)
    r = run_bass_kernel_spmd(nc, [arrays], core_ids=[0])
    return r.results[0]["out"]
```

```python
from contextlib import ExitStack

import concourse.bass as bass
from concourse import mybir

P = 128
F32 = mybir.dt.float32
I32 = mybir.dt.int32
U32 = mybir.dt.uint32
F32R = mybir.dt.float32r
ALU = mybir.AluOpType
ACT = mybir.ActivationFunctionType

B, H, L = 128, 32, 512
N = 64
E, I, TOPK = 16, 256, 4
KT = L // P
IT = I // P
VLEN, ULEN = 32, 16
SLOTS = B * H * TOPK
NT = (SLOTS + E * (P - 1)) // P
PACK = 8
PULL = 1
NROT, SHARED = 3, 3
WF, CH = 3072, 1024
F16 = mybir.dt.float16
AX = mybir.AxisListType.X
KPITCH = 640
GH = 4
NG = H // GH

TWO_PI = 6.283185307179586
C1, C2 = 6.28125, 0.00193500518798828125
C3 = TWO_PI - C1 - C2
LN2_HI, LN2_LO = 0.693359375, -2.12194440054690583e-4
ROUND = 12582912.0


class Count:

    def __init__(self, sem):
        self.sem, self.n = sem, 0

    def by(self, instruction, k=1):
        instruction.then_inc(self.sem, k)
        self.n += k
        return self.sem, self.n


def wait(engine, *marks):
    for sem, n in marks:
        engine.wait_ge(sem, n)


def build(nc, x, xT, lens, log_dt, c_re, c_im, log_a, a_im, d_skip, gate_w, bias, w_all, out, kpad, yrow):
    with ExitStack() as ctx:
        def sb(name, shape, dt=F32):
            return ctx.enter_context(nc.sbuf_tensor(name, shape, dt))

        def count(name):
            return Count(ctx.enter_context(nc.semaphore(name)))

        banks = ctx.enter_context(nc.psum_tensor("banks", [P, 8, 512], F32))
        TABLES = H * 4 * (VLEN + 2 * ULEN + 2)
        GROUP = KT * GH * B
        area = sb("area", [P, TABLES + 2 * GROUP])
        arena = area[:, 0:TABLES]
        with nc.sbuf_tensor("early_hi", [P, NROT * WF], F32) as early_hi:
            pass
        w_hi = sb("w_hi", [P, NROT + 1, WF], F32R)
        with nc.sbuf_tensor("early_lo", [P, NROT * WF], F32) as early_lo:
            pass
        w_lo = sb("w_lo", [P, NROT + 1, WF], F32R)
        raw0 = sb("raw0", [P, WF])
        pe, act, dve, pool = nc.tensor, nc.scalar, nc.vector, nc.gpsimd
        c_pe, c_act, c_dve, c_pool = count("c_pe"), count("c_act"), count("c_dve"), count("c_pool")

        def v(ins):
            m = c_dve.by(ins)
            wait(dve, m)
            return m

        par = sb("par", [P, 6, H])
        d_row = sb("d_row", [1, H])
        len_i = sb("len_i", [P, 1], I32)
        row_i = sb("row_i", [P, L])
        part_f = sb("part_f", [P, 1])
        gate_sb = sb("gate_sb", [P, KT, E])
        bias_sb = sb("bias_sb", [P, E])
        zero = sb("zero", [P, P])
        c_par, c_gate = count("c_par"), count("c_gate")
        nc.sync.dma_start(par[:, 0, :], log_dt.partition_broadcast(P)).then_inc(c_par.sem, 16)
        for half in range(2):
            q = slice(N * half, N * half + N)
            for j, src in ((1, log_a), (2, a_im), (3, c_re), (4, c_im)):
                nc.sync.dma_start(par[q, j, :], src).then_inc(c_par.sem, 16)
        c_par.n = 16 * 9
        m_par = (c_par.sem, c_par.n)
        m_d = c_gate.by(nc.scalar.dma_start(d_row[:], d_skip), 16)
        c_gate.by(nc.scalar.dma_start(len_i[:], lens), 16)
        c_gate.by(nc.scalar.dma_start(gate_sb[:], gate_w), 16)
        m_gate = c_gate.by(nc.scalar.dma_start(bias_sb[:], bias.partition_broadcast(P)), 16)

        c_init = count("c_init")
        c_raw = [[count(f"c_raw{q}_{c}") for c in range(3)] for q in range(3)]
        shared_in = [c_raw[0][c].by(nc.sync.dma_start(raw0[:, c * CH:(c + 1) * CH], w_all[E, :, c * CH:(c + 1) * CH]), 16)
                     for c in range(3)]

        NJ = VLEN + 2 * ULEN + 2
        X0, Y0, S1, SH = VLEN, VLEN + ULEN, NJ - 2, NJ - 1
        l_tab = sb("l_tab", [P, NJ])
        q_tab = sb("q_tab", [P, NJ])
        c_pool.by(pool.iota(l_tab[:, 0:VLEN], [[1, VLEN]], base=0, channel_multiplier=0, allow_small_or_imprecise_dtypes=True))
        c_pool.by(pool.iota(l_tab[:, X0:S1].rearrange("p (k a) -> p k a", k=2), [[0, 2], [VLEN, ULEN]], base=0,
                            channel_multiplier=0, allow_small_or_imprecise_dtypes=True))
        m_iota = (c_pool.sem, c_pool.n)
        c_pool.by(pool.iota(part_f[:], [[0, 1]], base=0, channel_multiplier=1, allow_small_or_imprecise_dtypes=True))
        m_row = c_pool.by(pool.iota(row_i[:], [[1, L]], base=0, channel_multiplier=0, allow_small_or_imprecise_dtypes=True))
        dve.memset(l_tab[:, S1:SH], 1.0)
        dve.memset(l_tab[:, SH:NJ], 0.5)
        for lo, quarters in ((0, (1, 1, 2)), (N, (0, 2, 3))):
            q = slice(lo, lo + N)
            dve.memset(q_tab[q, 0:X0], quarters[0] / 4)
            dve.memset(q_tab[q, X0:Y0], quarters[1] / 4)
            dve.memset(q_tab[q, Y0:S1], quarters[2] / 4)
        dve.memset(q_tab[:, S1:NJ], 0.0)
        m_zero = v(dve.memset(zero[:], 0.0))
        wait(nc.scalar, m_zero)
        for j in range(KT):
            m_init = c_init.by(nc.scalar.dma_start(out[H * B:, j * P:(j + 1) * P], zero[:]), 16)

        area2 = sb("area2", [P, 24 * 2 * H + H * VLEN])
        sm = area2[:, 0:24 * 2 * H].rearrange("p (j w) -> p j w", j=24)
        sm_i = sb("sm_i", [P, 2 * H], I32)

        def accurate_exp(dst, dst_m1, src, w):
            t, k, r, q, s = (sm[:, 16 + j, 0:w] for j in range(5))
            v(dve.tensor_scalar(t, src, -87.0, 88.0, ALU.max, ALU.min))
            v(dve.tensor_scalar(k, t, 1.4426950408889634, ROUND, ALU.mult, ALU.add))
            v(dve.tensor_scalar(k, k, ROUND, None, ALU.subtract))
            v(dve.scalar_tensor_tensor(out=r, in0=k, scalar=-LN2_HI, in1=t, op0=ALU.mult, op1=ALU.add))
            v(dve.scalar_tensor_tensor(out=r, in0=k, scalar=-LN2_LO, in1=r, op0=ALU.mult, op1=ALU.add))
            v(dve.tensor_scalar(q, r, 1 / 5040, None, ALU.mult))
            for c in (1 / 720, 1 / 120, 1 / 24, 1 / 6, 0.5, 1.0):
                v(dve.scalar_tensor_tensor(out=q, in0=q, scalar=c, in1=r, op0=ALU.add, op1=ALU.mult))
            v(dve.tensor_scalar(sm_i[:, 0:w], k, 127.0, 8388608.0, ALU.add, ALU.mult))
            two_k = sm_i[:, 0:w].bitcast(F32)
            v(dve.tensor_tensor(q, q, two_k, ALU.mult))
            if dst_m1 is not None:
                v(dve.tensor_scalar(s, two_k, -1.0, None, ALU.add))
                v(dve.tensor_tensor(dst_m1, q, s, ALU.add))
            return v(dve.tensor_tensor(dst, q, two_k, ALU.add))

        wait(dve, m_par)
        exps = sm[:, 0, :]
        accurate_exp(exps, None, par[:, 0:2, :].rearrange("p a h -> p (a h)"), 2 * H)
        dt, neg_are = sm[:, 0, 0:H], sm[:, 0, H:2 * H]
        aim = par[:, 2, :]
        are, d_re, d_im = sm[:, 1, 0:H], sm[:, 2, 0:H], sm[:, 3, 0:H]
        v(dve.tensor_scalar(are, neg_are, -1.0, None, ALU.mult))
        v(dve.tensor_tensor(d_re, are, dt, ALU.mult))
        v(dve.tensor_tensor(d_im, aim, dt, ALU.mult))

        NM = VLEN + ULEN
        ang = arena[:, 0:H * NJ].rearrange("p (h j) -> p h j", h=H)
        turns = arena[:, H * NJ:2 * H * NJ].rearrange("p (h j) -> p h j", h=H)
        sin = arena[:, 2 * H * NJ:3 * H * NJ].rearrange("p (h j) -> p h j", h=H)
        mag = arena[:, 3 * H * NJ:3 * H * NJ + H * NM].rearrange("p (h j) -> p h j", h=H)
        wide = [P, H, NJ]
        wait(dve, m_iota)
        m_mag = v(dve.tensor_tensor(mag, d_re.unsqueeze(2).to_broadcast([P, H, NM]),
                                    l_tab[:, 0:NM].unsqueeze(1).to_broadcast([P, H, NM]), ALU.mult))
        wait(act, m_mag)
        m_mag = c_act.by(act.activation(mag, mag, ACT.Exp))
        v(dve.tensor_tensor(ang, d_im.unsqueeze(2).to_broadcast(wide), l_tab[:].unsqueeze(1).to_broadcast(wide), ALU.mult))
        q_wide = q_tab[:].unsqueeze(1).to_broadcast(wide)
        v(dve.scalar_tensor_tensor(out=turns, in0=ang, scalar=1 / TWO_PI, in1=q_wide, op0=ALU.mult, op1=ALU.add))
        v(dve.tensor_scalar(turns, turns, ROUND, ROUND, ALU.add, ALU.subtract))
        for part in (C1, C2, C3):
            v(dve.scalar_tensor_tensor(out=ang, in0=turns, scalar=-part, in1=ang, op0=ALU.mult, op1=ALU.add))
        v(dve.scalar_tensor_tensor(out=ang, in0=q_wide, scalar=TWO_PI, in1=ang, op0=ALU.mult, op1=ALU.add))
        m_ang = v(dve.tensor_scalar(ang, ang, 3.1415925, -3.1415925, ALU.min, ALU.max))
        wait(act, m_ang)
        m_sin = c_act.by(act.activation(sin, ang, ACT.Sin))

        ew, em = sm[:, 4, 0:H], sm[:, 5, 0:H]
        accurate_exp(ew, em, d_re, H)
        t0, t1, nr, ni, rd, gr, gi, ctr, cti = (sm[:, 6 + j, 0:H] for j in range(9))
        v(dve.tensor_tensor(t0, are, are, ALU.mult))
        v(dve.tensor_tensor(t1, aim, aim, ALU.mult))
        v(dve.tensor_tensor(t0, t0, t1, ALU.add))
        v(dve.tensor_scalar(t0, t0, 0.5, None, ALU.mult))
        v(dve.reciprocal(rd, t0))
        wait(dve, m_sin)
        s_one, s_half = sin[:, :, S1], sin[:, :, SH]
        v(dve.scalar_tensor_tensor(out=t0, in0=s_half, scalar=2.0, in1=s_half, op0=ALU.mult, op1=ALU.mult))
        v(dve.tensor_tensor(t0, t0, ew, ALU.mult))
        v(dve.tensor_tensor(nr, em, t0, ALU.subtract))
        v(dve.tensor_tensor(ni, ew, s_one, ALU.mult))
        for dst, a, b_, op in ((gr, (nr, are), (ni, aim), ALU.add), (gi, (ni, are), (nr, aim), ALU.subtract)):
            v(dve.tensor_tensor(t0, *a, ALU.mult))
            v(dve.tensor_tensor(t1, *b_, ALU.mult))
            v(dve.tensor_tensor(t0, t0, t1, op))
            v(dve.tensor_tensor(dst, t0, rd, ALU.mult))
        cre, cim = par[:, 3, :], par[:, 4, :]
        for dst, a, b_, op in ((ctr, (cre, gr), (cim, gi), ALU.subtract), (cti, (cre, gi), (cim, gr), ALU.add)):
            v(dve.tensor_tensor(t0, *a, ALU.mult))
            v(dve.tensor_tensor(t1, *b_, ALU.mult))
            v(dve.tensor_tensor(dst, t0, t1, op))
        u_wide = [P, H, ULEN]
        u_x, u_y = sin[:, :, X0:Y0], sin[:, :, Y0:S1]
        v(dve.tensor_tensor(u_x, u_x, ctr.unsqueeze(2).to_broadcast(u_wide), ALU.mult))
        v(dve.tensor_tensor(u_y, u_y, cti.unsqueeze(2).to_broadcast(u_wide), ALU.mult))
        v(dve.tensor_tensor(u_x, u_x, u_y, ALU.add))
        wait(dve, m_mag)
        v(dve.tensor_tensor(u_x, u_x, mag[:, :, VLEN:NM], ALU.mult))
        m_uv = v(dve.tensor_tensor(sin[:, :, 0:VLEN], sin[:, :, 0:VLEN], mag[:, :, 0:VLEN], ALU.mult))

        wait(pe, m_uv)
        for h in range(H):
            k_ps = banks[0:ULEN, 4 + h // 16, (h % 16) * VLEN:(h % 16 + 1) * VLEN]
            mm = pe.matmul(k_ps, u_x[:, h, :], sin[:, h, 0:VLEN], start=True, stop=True)
        m_k = c_pe.by(mm)
        k_sb = area2[0:ULEN, 24 * 2 * H:].rearrange("a (h b) -> a h b", h=H)
        wait(dve, m_k)
        v(dve.tensor_copy(k_sb.rearrange("a (g h) b -> a g (h b)", g=2), banks[0:ULEN, 4:6, :]))
        wait(dve, m_gate)
        m_ksb = v(dve.tensor_tensor(k_sb[0:1, :, 0], k_sb[0:1, :, 0], d_row[:], ALU.add))
        c_kpad = count("c_kpad")
        kh = kpad.tensor
        wait(nc.sync, m_zero)
        c_kpad.by(nc.sync.dma_start(bass.AP(kh, 0, [[KPITCH, H], [1, P - 1]]), zero[0:H, 0:P - 1]), 16)
        wait(nc.sync, m_ksb)
        m_kpad = c_kpad.by(nc.sync.dma_start(bass.AP(kh, P - 1, [[VLEN, ULEN], [KPITCH, H], [1, VLEN]]), k_sb), 16)

        ident = sb("ident", [P, P])
        len_f = sb("len_f", [P, 1])
        wait(dve, m_row)
        v(dve.tensor_copy(len_f[:], len_i[:]))
        m_ident = v(dve.tensor_scalar(ident[:], row_i[:, 0:P], part_f[:, 0:1], None, ALU.is_equal))

        NR = 2
        taps = area[:, 0:NR * GROUP].rearrange("p (r h c) -> p r h c", r=NR, h=GH)
        xin = area[:, TABLES:].rearrange("p (r k t) -> p r k t", r=NR, k=KT)
        y_row = area2[:, 0:3 * L].rearrange("p (r l) -> p r l", r=3)
        small = sb("small", [P, 2, L])
        c_taps = [count(f"c_taps{i}") for i in range(NR)]
        c_xin = [count(f"c_xin{i}") for i in range(NR)]
        c_yst = [count(f"c_yst{i}") for i in range(3)]
        loaded, used, rows, stored, turned, evac = {}, {}, {}, {}, {}, {}

        sc = sb("sc", [P, H, E])
        top = sb("top", [P, H, 8])
        idx = sb("idx", [P, H, 8], U32)
        idx_f = sb("idx_f", [P, H, TOPK])
        wt = sb("wt", [P, H, TOPK])
        ssum = sb("ssum", [P, H])
        hot = early_lo[:, 0:TOPK * H * E].rearrange("p (k c e) -> p k c e", k=TOPK, c=H)
        cw = small[:, 0, :].rearrange("p (c e) -> p c e", c=H)
        rank = small[:, 1, :].rearrange("p (c e) -> p c e", c=H)
        IN_HI = NROT * WF // L

        def y_t(c):
            if c < IN_HI:
                return early_hi[:, c * L:(c + 1) * L]
            at_ = TOPK * H * E + (c - IN_HI) * L
            return early_lo[:, at_:at_ + L]

        tmp = sc
        picked = sb("picked", [P, H, E], F16)
        ones16 = sb("ones16", [P, P], F16)
        before16 = sb("before16", [P, P], F16)
        token1 = sb("token1", [P, H])
        v(dve.memset(ones16[:], 1.0))
        v(dve.tensor_scalar(before16[:], row_i[:, 0:P], part_f[:, 0:1], None, ALU.is_gt))
        v(dve.tensor_scalar(token1[:], row_i[:, 0:H], float(P), 1.0, ALU.mult, ALU.add))
        v(dve.tensor_scalar(token1[:, H // 2:], token1[:, H // 2:], -2048.0, None, ALU.add))
        v(dve.tensor_scalar(token1[:], token1[:], part_f[:, 0:1], None, ALU.add))

        logits, scored = {}, {}

        def choose(c0):
            cs = slice(c0, c0 + GH)
            some = [P, GH, E]
            wait(act, logits[c0 + GH - 1])
            m = c_act.by(act.activation(sc[:, cs], banks[:, 6 + c0 // GH % 2, 0:GH * E].rearrange("p (c e) -> p c e", c=GH), ACT.Sigmoid))
            scored[c0] = m
            wait(dve, m)
            v(dve.tensor_tensor(sc[:, cs], sc[:, cs], bias_sb[:].unsqueeze(1).to_broadcast(some), ALU.add))
            for c in range(c0, c0 + GH):
                m = c_dve.by(dve.max(top[:, c, :], sc[:, c, :]))
            wait(dve, m)
            for c in range(c0, c0 + GH):
                m = c_dve.by(dve.max_index(idx[:, c, :], top[:, c, :], sc[:, c, :]))
            wait(dve, m)
            v(dve.tensor_copy(idx_f[:, cs], idx[:, cs, 0:TOPK]))
            for k in range(TOPK):
                m = c_dve.by(dve.tensor_tensor(hot[:, k, cs], row_i[:, 0:E].unsqueeze(1).to_broadcast(some),
                                               idx_f[:, cs, k:k + 1].to_broadcast(some), ALU.is_equal))
            wait(dve, m)

        def weigh(c0):
            cs = slice(c0, c0 + GH)
            some = [P, GH, E]
            v(dve.tensor_tensor(tmp[:, cs], hot[:, 0, cs], hot[:, 1, cs], ALU.add))
            v(dve.tensor_tensor(tmp[:, cs], tmp[:, cs], hot[:, 2, cs], ALU.add))
            m_picked = v(dve.tensor_tensor(picked[:, cs], tmp[:, cs], hot[:, 3, cs], ALU.add))
            v(dve.tensor_reduce(ssum[:, cs], top[:, cs, 0:TOPK], AX, ALU.add))
            v(dve.tensor_scalar(ssum[:, cs], ssum[:, cs], 1e-20, None, ALU.add))
            v(dve.reciprocal(ssum[:, cs], ssum[:, cs]))
            v(dve.tensor_tensor(wt[:, cs], top[:, cs, 0:TOPK], ssum[:, cs].unsqueeze(2).to_broadcast([P, GH, TOPK]), ALU.mult))
            m_cw = v(dve.tensor_tensor(cw[:, cs], hot[:, 0, cs], wt[:, cs, 0:1].to_broadcast(some), ALU.mult))
            for k in range(1, TOPK):
                v(dve.tensor_tensor(tmp[:, cs], hot[:, k, cs], wt[:, cs, k:k + 1].to_broadcast(some), ALU.mult))
                m_cw = v(dve.tensor_tensor(cw[:, cs], cw[:, cs], tmp[:, cs], ALU.add))
            return m_picked, m_cw

        def load_inputs(g):
            r = g % NR
            if g >= NR:
                wait(nc.sync, used[g - NR])
            m = c_xin[r].by(nc.sync.dma_start(xin[:, r], xT[:, :, g * GH * B:(g + 1) * GH * B].rearrange("m p t -> p m t")), 16)
            if g == 0:
                wait(nc.sync, m_kpad)
            loaded[g] = (m, c_taps[r].by(nc.sync.dma_start(
                taps[:, r], bass.AP(kh, KPITCH * GH * g, [[1, P], [KPITCH, GH], [1, 512]])), 16))

        for g in range(NR):
            load_inputs(g)
        wait(pe, m_gate, m_ident)
        shared_split = {}
        for h in range(H + 4):
            if h < H:
                g, r = h // GH, (h // GH) % NR
                if h % GH == 0:
                    wait(pe, *loaded[g])
                if h >= 3:
                    wait(pe, rows[h - 3])
                for m_ in range(KT):
                    mm = pe.matmul(banks[:, h % 3, m_ * P:512], xin[:, r, m_, (h % GH) * B:(h % GH + 1) * B],
                                   taps[:, r, h % GH, 0:512 - m_ * P], start=(m_ == 0), stop=(m_ == KT - 1))
                m = c_pe.by(mm)
                if h % GH == GH - 1:
                    used[g] = m
                    if g + NR < NG:
                        load_inputs(g + NR)
                wait(dve, m)
                if h >= 3:
                    wait(dve, stored[h - 3], turned[h - 3])
                rows[h] = c_dve.by(dve.scalar_tensor_tensor(
                    out=y_row[:, h % 3, :], in0=row_i[:], scalar=len_f[:, 0:1], in1=banks[:, h % 3, :], op0=ALU.is_lt, op1=ALU.mult))
                wait(nc.scalar, rows[h])
                stored[h] = c_yst[h % 3].by(nc.scalar.dma_start(yrow[h * B:(h + 1) * B, 0:L], y_row[:, h % 3, :]), 16)
            if 1 <= h <= H:
                c = h - 1
                wait(pe, rows[c])
                if c >= 2:
                    wait(pe, evac[c - 2])
                for j in range(KT):
                    mm = pe.transpose(banks[:, 3 + c % 2, j * P:(j + 1) * P], y_row[:, c % 3, j * P:(j + 1) * P], ident[:])
                turned[c] = c_pe.by(mm)
                wait(act, turned[c])
                evac[c] = c_act.by(act.copy(y_t(c), banks[:, 3 + c % 2, :]))
            if h in (4, 8, 12):
                c = h // 4 - 1
                cs = slice(c * CH, (c + 1) * CH)
                wait(act, shared_in[c])
                m = c_act.by(act.copy(w_hi[:, SHARED, cs], raw0[:, cs]))
                wait(dve, m, shared_in[c])
                shared_split[c] = (m, c_dve.by(dve.tensor_tensor(w_lo[:, SHARED, cs], raw0[:, cs], w_hi[:, SHARED, cs].bitcast(F32), ALU.subtract)))
            if 2 <= h < H + 2:
                c = h - 2
                wait(pe, evac[c])
                if c % GH == 0 and c >= 2 * GH:
                    wait(pe, scored[c - 2 * GH])
                for j in range(KT):
                    mm = pe.matmul(banks[:, 6 + c // GH % 2, c % GH * E:(c % GH + 1) * E], y_t(c)[:, j * P:(j + 1) * P], gate_sb[:, j, :],
                                   start=(j == 0), stop=(j == KT - 1))
                logits[c] = c_pe.by(mm)
            if h >= GH + 1 and h % GH == 1:
                choose(h - 1 - GH)
            if GH + 3 <= h < H + 3 and h % GH == 3:
                weigh(h - 3 - GH)

        NM8 = -(-NT // PACK) * PACK
        at = [0]

        def part(*shape):
            n = 1
            for d in shape:
                n *= d
            at[0] += n
            names = "abc"[:len(shape)]
            return area[:, at[0] - n:at[0]].rearrange(f"p ({' '.join(names)}) -> p {' '.join(names)}", **dict(zip(names, shape)))

        raw = [raw0[:], part(WF), part(WF)]
        rows_in = part(3, L + E)
        add_in = part(2, L)
        silu = part(2, I)
        z = part(2, I)
        o_sb = part(3, L)
        cum = sb("cum", [P, 2, 2 * E])
        ordn = sb("ordn", [P, 2, 2 * E])
        used_e = sb("used_e", [P, E])
        slot = sb("slot", [P, H, TOPK])
        slot_a = sb("slot_a", [P, H, TOPK], F16)
        slot_b = sb("slot_b", [P, H, TOPK], F16)
        slot_t = sb("slot_t", [P, H, TOPK])
        g_idx = sb("g_idx", [P, NT], I32)
        s_idx = sb("s_idx", [P, NT], I32)
        tok = sb("tok", [P, NT])
        upper = sb("upper", [P, NT])
        tile_e = sb("tile_e", [P, NT])
        tile_hot = sb("tile_hot", [P, NT, E], F16)
        meta = sb("meta", [1, 2, NT + 2], I32)
        meta_f = raw[1][0:1, WF - 4 * (NM8 + 2):].rearrange("p (r t) -> p r t", r=4)
        packed = sb("packed", [1, 2, NM8 // PACK], I32)
        packed_f = sb("packed_f", [1, 2, NM8 // PACK])
        place = sb("place", [1, 2, PACK])
        c_cw = count("c_cw")
        c_meta = count("c_meta")
        full = [P, H, E]
        marks = {}

        def routing():
            m_picked, m_cw = weigh(H - GH)
            wait(nc.sync, m_cw)
            marks["cw"] = c_cw.by(nc.sync.dma_start(yrow[:, L:L + E].rearrange("(c p) e -> p c e", p=P), cw[:]), 16)
            wait(pe, m_picked)
            mm = pe.matmul(banks[:, 5, :], before16[:], picked[:].rearrange("p c e -> p (c e)"), start=True, stop=False)
            for c in range(H - 1):
                mm = pe.matmul(banks[:, 5, (c + 1) * E:512], ones16[:], picked[:, c:c + 1, :].to_broadcast([P, H - 1 - c, E]),
                               start=False, stop=(c == H - 2))
            for c in range(H):
                mm = pe.matmul(banks[:, 7, 0:E], ones16[:], picked[:, c, :], start=(c == 0), stop=(c == H - 1))
            m_rank = c_pe.by(mm)
            yield

            wait(dve, m_rank)
            v(dve.memset(cum[:], 0.0))
            v(dve.memset(ordn[:], 0.0))
            v(dve.tensor_scalar(used_e[:], banks[:, 7, 0:E], 0.0, None, ALU.is_gt))
            v(dve.tensor_copy(ordn[:, 0, E:], used_e[:]))
            v(dve.tensor_scalar(cum[:, 0, E:], banks[:, 7, 0:E], P / 2 - 0.5, 1 / P, ALU.add, ALU.mult))
            v(dve.tensor_scalar(cum[:, 0, E:], cum[:, 0, E:], ROUND, ROUND, ALU.add, ALU.subtract))
            yield
            for n, d in enumerate((1, 2, 4, 8)):
                v(dve.tensor_tensor(cum[:, (n + 1) % 2, E:], cum[:, n % 2, E:], cum[:, n % 2, E - d:2 * E - d], ALU.add))
                v(dve.tensor_tensor(ordn[:, (n + 1) % 2, E:], ordn[:, n % 2, E:], ordn[:, n % 2, E - d:2 * E - d], ALU.add))
                if n == 1:
                    yield
            yield
            cum_incl, cum_excl = cum[:, 0, E:2 * E], cum[:, 0, E - 1:2 * E - 1]
            v(dve.scalar_tensor_tensor(out=rank[:], in0=cum_excl.unsqueeze(1).to_broadcast(full), scalar=float(P),
                                       in1=banks[:, 5, :].rearrange("p (c e) -> p c e", c=H), op0=ALU.mult, op1=ALU.add))
            yield
            for k in range(TOPK):
                v(dve.tensor_tensor(tmp[:], hot[:, k], rank[:], ALU.mult))
                v(dve.tensor_reduce(slot[:, :, k], tmp[:], AX, ALU.add))
                yield
            v(dve.tensor_scalar(slot_t[:], slot[:], -(P / 2 - 0.5), 1 / P, ALU.add, ALU.mult))
            v(dve.tensor_scalar(slot_t[:], slot_t[:], ROUND, ROUND, ALU.add, ALU.subtract))
            v(dve.tensor_copy(slot_a[:], slot_t[:]))
            m_slot = v(dve.scalar_tensor_tensor(out=slot_b[:], in0=slot_t[:], scalar=-float(P), in1=slot[:], op0=ALU.mult, op1=ALU.add))
            yield

            NP_ = 2 * TOPK
            pair = [P, 1, NP_]
            flat = [t.bitcast(F16) for t in (raw[1], raw[2])]
            row_wide = flat[0][:, 0:(NT + 1) * NP_].rearrange("p (r n) -> p r n", n=NP_)
            o = (NT + 1) * NP_
            b_hot = [flat[1][:, q * P * NP_:(q + 1) * P * NP_].rearrange("p (r n) -> p r n", n=NP_) for q in range(2)]
            a_hot = [flat[0][:, o + q * o:2 * o + q * o].rearrange("p (r n) -> p r n", n=NP_) for q in range(2)]
            o2 = 2 * P * NP_
            a_tok = [flat[1][:, o2 + q * o:o2 + o + q * o].rearrange("p (r n) -> p r n", n=NP_) for q in range(2)]
            v(dve.tensor_copy(row_wide, row_i[:, 0:NT + 1].unsqueeze(2).to_broadcast([P, NT + 1, NP_])))
            yield
            freed, scaled, b_ready = {}, {}, {}
            NBATCH = H * TOPK // NP_

            def products(n):
                q, c0 = n % 2, 2 * n
                half = c0 // (H // 2)
                wait(pe, scaled[n], b_ready[n])
                for i in range(NP_):
                    first = n % (NBATCH // 2) == 0 and i == 0
                    last = n % (NBATCH // 2) == NBATCH // 2 - 1 and i == NP_ - 1
                    mm = pe.matmul(banks[:, (5, 7)[half], 0:NT + 1], b_hot[q][:, :, i], a_tok[q][:, :, i], start=first, stop=last)
                freed[n] = c_pe.by(mm)

            for n in range(NBATCH):
                q, c0 = n % 2, 2 * n
                if n >= 2:
                    wait(dve, freed[n - 2])
                    wait(act, freed[n - 2])
                sa, sb_ = (t[:, c0:c0 + 2, :].rearrange("p c k -> p (c k)").unsqueeze(1) for t in (slot_a, slot_b))
                if n >= 2:
                    wait(dve, scaled[n - 2])
                m = c_dve.by(dve.tensor_tensor(a_hot[q], row_wide, sa.to_broadcast([P, NT + 1, NP_]), ALU.is_equal))
                wait(act, m)
                for i in range(2):
                    ks = slice(i * TOPK, (i + 1) * TOPK)
                    ma = c_act.by(act.activation(a_tok[q][:, :, ks], a_hot[q][:, :, ks], ACT.Copy, scale=token1[:, c0 + i:c0 + i + 1]))
                mb = c_dve.by(dve.tensor_tensor(b_hot[q], row_wide[:, 0:P, :], sb_.to_broadcast([P, P, NP_]), ALU.is_equal))
                scaled[n], b_ready[n] = ma, mb
                yield
                products(n)
            yield
            wait(dve, freed[NBATCH - 1])
            v(dve.tensor_scalar(upper[:], banks[:, 7, 0:NT], 0.0, 2048.0, ALU.is_gt, ALU.mult))
            v(dve.tensor_tensor(upper[:], upper[:], banks[:, 7, 0:NT], ALU.add))
            v(dve.tensor_tensor(tok[:], upper[:], banks[:, 5, 0:NT], ALU.add))
            yield
            marks["gather"] = v(dve.tensor_scalar(g_idx[:], tok[:], -1.0, 0.0, ALU.add, ALU.max))
            v(dve.tensor_scalar(upper[:], tok[:], 0.0, float(H * B + 1), ALU.is_equal, ALU.mult))
            v(dve.tensor_tensor(tok[:], tok[:], upper[:], ALU.add))
            v(dve.tensor_scalar(upper[:], upper[:], 0.0, part_f[:, 0:1], ALU.is_gt, ALU.mult))
            marks["scatter"] = v(dve.scalar_tensor_tensor(out=s_idx[:], in0=tok[:], scalar=-1.0, in1=upper[:], op0=ALU.add, op1=ALU.add))
            yield

            last_e = ssum[:, 0:1]
            HALVES = (slice(0, NT // 2), slice(NT // 2, NT))
            for t in HALVES:
                wide_h = [P, t.stop - t.start, E]
                v(dve.tensor_tensor(tile_hot[:, t], row_i[:, t].unsqueeze(2).to_broadcast(wide_h), cum_incl.unsqueeze(1).to_broadcast(wide_h), ALU.is_ge))
                yield
            for t in HALVES:
                v(dve.tensor_reduce(tile_e[:, t], tile_hot[:, t], AX, ALU.add))
                yield
            v(dve.tensor_tensor(sc[:, 0, :], used_e[:], row_i[:, 0:E], ALU.mult))
            v(dve.tensor_reduce(last_e, sc[:, 0, :], AX, ALU.max))
            v(dve.tensor_scalar(tile_e[:], tile_e[:], last_e, None, ALU.min))
            yield
            for t in HALVES:
                wide_h = [P, t.stop - t.start, E]
                v(dve.tensor_tensor(tile_hot[:, t], tile_e[:, t].unsqueeze(2).to_broadcast(wide_h), row_i[:, 0:E].unsqueeze(1).to_broadcast(wide_h), ALU.is_equal))
                yield
            one = [1, NT, E]
            big = upper2
            v(dve.tensor_tensor(big, tile_hot[0:1], ordn[0:1, 0, E - 1:2 * E - 1].unsqueeze(1).to_broadcast(one), ALU.mult))
            yield
            v(dve.tensor_reduce(meta_f[:, 0, 2:NT + 2], big, AX, ALU.add))
            yield
            v(dve.memset(meta_f[:, 0, NT + 2:], 0.0))
            v(dve.tensor_scalar(meta_f[:, 0, 2:], meta_f[:, 0, 2:], 2.0, None, ALU.add))
            v(dve.tensor_copy(meta_f[:, 0, 0:2], row_i[0:1, 0:2]))
            v(dve.tensor_scalar(meta_f[:, 3, :], meta_f[:, 0, :], -1.0, 1 / 3, ALU.add, ALU.mult))
            v(dve.tensor_scalar(meta_f[:, 3, :], meta_f[:, 3, :], ROUND, ROUND, ALU.add, ALU.subtract))
            v(dve.scalar_tensor_tensor(out=meta_f[:, 3, :], in0=meta_f[:, 3, :], scalar=-3.0, in1=meta_f[:, 0, :], op0=ALU.mult, op1=ALU.add))
            v(dve.tensor_scalar(meta_f[:, 2, :], meta_f[:, 3, :], 2.0, -3.0, ALU.is_equal, ALU.mult))
            v(dve.scalar_tensor_tensor(out=meta_f[:, 2, :], in0=meta_f[:, 3, :], scalar=1.0, in1=meta_f[:, 2, :], op0=ALU.add, op1=ALU.add))
            v(dve.memset(meta_f[:, 1, :], 1.0))
            v(dve.tensor_tensor(meta_f[:, 1, 3:NT + 2], tile_e[0:1, 1:], tile_e[0:1, 0:NT - 1], ALU.not_equal))
            yield
            yield
            for i in range(PACK):
                dve.memset(place[:, 0, i:i + 1], float(4 ** i))
                m = c_dve.by(dve.memset(place[:, 1, i:i + 1], float(8 ** i)))
            wait(dve, m)
            v(dve.scalar_tensor_tensor(out=meta_f[:, 3, :], in0=meta_f[:, 1, :], scalar=4.0, in1=meta_f[:, 3, :], op0=ALU.mult, op1=ALU.add))
            yield
            four = [1, 2, NM8 // PACK, PACK]
            digits = meta_f[:, 2:4, 2:].rearrange("p r (g i) -> p r g i", i=PACK)
            v(dve.tensor_tensor(digits, digits, place[:].unsqueeze(2).to_broadcast(four), ALU.mult))
            v(dve.tensor_reduce(packed_f[:], digits, AX, ALU.add))
            v(dve.tensor_copy(packed[:], packed_f[:]))
            yield
            one2 = [1, NT + 2, E]
            v(dve.tensor_tensor(big2, meta_f[:, 0, 0:NT + 2].unsqueeze(2).to_broadcast(one2), ordn[0:1, 0, E - 1:2 * E - 1].unsqueeze(1).to_broadcast(one2), ALU.is_equal))
            yield
            v(dve.tensor_tensor(big2, big2, sc[0:1, 0:1, :].to_broadcast(one2), ALU.mult))
            yield
            v(dve.tensor_reduce(meta_f[:, 0, 0:NT + 2], big2, AX, ALU.add))
            marks["meta"] = v(dve.tensor_copy(meta[:], meta_f[:, 0:2, 0:NT + 2]))
            yield

        upper2 = raw[1][0:1, 0:NT * E].rearrange("p (t e) -> p t e", e=E)
        big2 = raw[1][0:1, 0:(NT + 2) * E].rearrange("p (t e) -> p t e", e=E)
        background = routing()

        def pull(n=1):
            for _ in range(n):
                next(background, None)

        yt_hi = sb("yt_hi", [P, 2, KT, P], F32R)
        yt_lo = sb("yt_lo", [P, 2, KT, P], F32R)
        zt_hi = sb("zt_hi", [P, 2, IT, P], F32R)
        zt_lo = sb("zt_lo", [P, 2, IT, P], F32R)
        w_tok = sb("w_tok", [P, 4])
        junk = sb("junk", [P, E])
        c_rg = [count(f"c_rg{i}") for i in range(3)]
        c_add = [count(f"c_add{i}") for i in range(2)]
        c_sa = [count(f"c_sa{i}") for i in range(3)]
        c_st = [count(f"c_st{i}") for i in range(3)]

        steps = [("shared", c) for c in range(H)] + [("expert", j) for j in range(NT)]
        NS = len(steps)
        E0 = H
        in_ready, add_ready = {}, {}
        ty, yh, yl, gu, si, zz, tz, zh, zl, dn, od, sent, wtk, added = ({} for _ in range(14))
        raw_in, split = {}, {}
        scattered = []

        def fetch(s):
            kind, n = steps[s]
            if kind == "shared":
                return
            r = s % 3
            if n >= 3:
                wait(pool, ty[s - 3], wtk[s - 3])
            if n == 0:
                wait(pool, marks["gather"], marks["cw"], *[stored[c] for c in range(H - 3, H)])
            in_ready[s] = c_rg[r].by(pool.indirect_dma_start(
                out=rows_in[:, r, :], out_offset=None, in_=yrow,
                in_offset=bass.IndirectOffsetOnAxis(ap=g_idx[:, n:n + 1], axis=0)), 16)

        def fetch_addend(s):
            if 0 <= s < H:
                if s == 0:
                    wait(nc.sync, used[NG - 1])
                if s >= 2:
                    wait(nc.sync, added[s - 2])
                add_ready[s] = c_add[s % 2].by(nc.sync.dma_start(add_in[:, s % 2, :], x[s * B:(s + 1) * B, :]), 16)

        to_load, starts, job_word, slot_word, hi_made = {}, {}, {}, {}, {}

        def job_fetch(j, c):
            if not -2 <= j < NT:
                return
            q = (j + 2) % 3
            cs = slice(c * CH, (c + 1) * CH)
            if (j - 3, c) in split:
                wait(nc.sync, *split[j - 3, c])
            if (j, c) in ((-2, 0), (-1, 0)):
                wait(nc.sync, marks["meta"])
            if c == 0:
                to_load[j] = nc.sync.value_load(meta[0:1, 0, j + 2:j + 3], min_val=0, max_val=E - 1)
                if j > 0:
                    starts[j] = nc.sync.value_load(meta[0:1, 1, j + 2:j + 3], min_val=0, max_val=1)
            e = to_load[j]
            src = w_all[bass.ds(e, 1), :, cs].rearrange("o p n -> (o p) n")
            if j <= 0:
                ins = nc.sync.dma_start(raw[q][:, cs], src)
            else:
                ins = nc.sync.dma_start(raw[q][:, cs], src, cond=starts[j])
            raw_in[j, c] = c_raw[q][c].by(ins, 16)

        def job_split(j, c):
            q = (j + 2) % 3
            cs = slice(c * CH, (c + 1) * CH)
            wait(act, raw_in[j, c], yl[H - 1 + j])
            m = c_act.by(act.copy(w_hi[:, q, cs], raw[q][:, cs]))
            wait(dve, raw_in[j, c], m)
            split[j, c] = (m, c_dve.by(dve.tensor_tensor(w_lo[:, q, cs], raw[q][:, cs], w_hi[:, q, cs].bitcast(F32), ALU.subtract)))

        def jobs_split(eng, t):
            first = t + 1 if eng is act else t
            todo = [(first - c, c) for c in range(3) if 1 <= first - c < NT]
            if not todo:
                return
            code = {}
            for j, c in todo:
                if eng is act:
                    wait(act, raw_in[j, c])
                    wait(act, gu[E0 + j - 1] if c < 2 else dn[E0 + j - 1])
                else:
                    wait(dve, raw_in[j, c], hi_made[j, c])
                g, i = divmod(j, PACK)
                if (eng, g) not in job_word:
                    job_word[eng, g] = eng.value_load(packed[0:1, 1, g:g + 1], min_val=0, max_val=8 ** PACK - 1)
                code[j] = (job_word[eng, g] >> (3 * i)) & 7
            some = code[todo[0][0]]
            for j, c in todo[1:]:
                some = some | code[j]
            with eng.If(some >= 4):
                for j, c in todo:
                    with eng.If(code[j] >= 4):
                        src = raw[(j + 2) % 3][:, c * CH:(c + 1) * CH]
                        hi, lo = (w[:].rearrange("p s n -> p (s n)")[:, bass.ds((code[j] & 3) * WF + c * CH, CH)] for w in (w_hi, w_lo))
                        if eng is act:
                            act.copy(hi, src)
                        else:
                            dve.tensor_tensor(lo, src, hi.bitcast(F32), ALU.subtract)
            m = (c_act if eng is act else c_dve).by(eng.drain())
            for j, c in todo:
                if eng is act:
                    hi_made[j, c] = m
                else:
                    split[j, c] = (hi_made[j, c], m)

        def turn_rows(s):
            if steps[s][0] == "shared":
                return
            r = s % 3
            wait(pe, in_ready[s])
            if s >= 2:
                wait(pe, yl[s - 2])
            for j in range(KT):
                mm = pe.transpose(banks[:, s % 2, j * P:(j + 1) * P], rows_in[:, r, j * P:(j + 1) * P], ident[:])
            ty[s] = c_pe.by(mm)

        def split_rows(s):
            kind, n = steps[s]
            rows_t = y_t(n) if kind == "shared" else banks[:, s % 2, :]
            wait(act, evac[n] if kind == "shared" else ty[s])
            if s >= 2:
                wait(act, gu[s - 2])
            hi, lo = (t[:, s % 2].rearrange("p j t -> p (j t)") for t in (yt_hi, yt_lo))
            yh[s] = c_act.by(act.copy(hi, rows_t))
            wait(dve, yh[s])
            yl[s] = c_dve.by(dve.tensor_tensor(lo, rows_t, hi.bitcast(F32), ALU.subtract))
            if kind == "expert":
                wait(dve, in_ready[s])
                if s >= 4 and s - 4 in od:
                    wait(dve, od[s - 4])
                wtk[s] = c_dve.by(dve.tensor_tensor_reduce(junk[:], rows_in[:, s % 3, L:L + E], tile_hot[:, n, :], 1.0, 0.0,
                                                           ALU.mult, ALU.add, w_tok[:, s % 4:s % 4 + 1]))
                wait(dve, wtk[s])

        slot_of = {}

        def weights(s, w, at_):
            if steps[s][0] != "expert":
                return w[:, SHARED, at_:at_ + 512]
            return w[:].rearrange("p s n -> p (s n)")[:, bass.ds(slot_of[s] * WF + at_, 512)]

        def up(s, half):
            kind, n = steps[s]
            b = 2 + s % 2
            if half == 0:
                if kind == "expert":
                    g, i = divmod(n, PACK)
                    if n == 0:
                        wait(pe, marks["meta"])
                    if i == 0:
                        slot_word[g] = pe.value_load(packed[0:1, 0, g:g + 1], min_val=0, max_val=4 ** PACK - 1)
                    slot_of[s] = (slot_word[g] >> (2 * i)) & 3
                wait(pe, yh[s])
                if s >= 2:
                    wait(pe, zz[s - 2])
            if kind == "expert":
                wait(pe, *split[n - 2, half])
            else:
                wait(pe, *shared_split[half])
            pair = (2 * half, 2 * half + 1)
            for j, yt, w in [(j, yt_hi, w) for j in pair for w in (w_hi, w_lo)] + [(j, yt_lo, w_hi) for j in pair]:
                if half == 0 and yt is yt_lo and j == 0:
                    wait(pe, yl[s])
                mm = pe.matmul(banks[:, b, :], yt[:, s % 2, j, :], weights(s, w, j * 512), start=(j == 0 and yt is yt_hi and w is w_hi),
                               stop=(j == KT - 1 and yt is yt_lo))
            if half:
                gu[s] = c_pe.by(mm)

        def activate(s):
            b = 2 + s % 2
            wait(act, gu[s])
            if s >= 2:
                wait(act, zz[s - 2])
            si[s] = c_act.by(act.activation(silu[:, s % 2, :], banks[:, b, 0:I], ACT.Silu))
            wait(dve, si[s])
            if s >= 2:
                wait(dve, tz[s - 2])
            zz[s] = c_dve.by(dve.tensor_tensor(z[:, s % 2, :], silu[:, s % 2, :], banks[:, b, I:2 * I], ALU.mult))

        def turn_z(s):
            wait(pe, zz[s])
            if s >= 1:
                wait(pe, zl[s - 1])
            for j in range(IT):
                mm = pe.transpose(banks[:, 4, j * P:(j + 1) * P], z[:, s % 2, j * P:(j + 1) * P], ident[:])
            tz[s] = c_pe.by(mm)

        def split_z(s):
            wait(act, tz[s])
            if s >= 2:
                wait(act, dn[s - 2])
            hi, lo = (t[:, s % 2].rearrange("p j t -> p (j t)") for t in (zt_hi, zt_lo))
            zh[s] = c_act.by(act.copy(hi, banks[:, 4, 0:I]))
            wait(dve, zh[s])
            zl[s] = c_dve.by(dve.tensor_tensor(lo, banks[:, 4, 0:I], hi.bitcast(F32), ALU.subtract))

        def down(s):
            kind, n = steps[s]
            b = 6
            wait(pe, zh[s])
            if s >= 1:
                wait(pe, od[s - 1])
            wait(pe, *(split[n - 2, 2] if kind == "expert" else shared_split[2]))
            for j, zt, w in [(j, zt_hi, w) for j in range(IT) for w in (w_hi, w_lo)] + [(j, zt_lo, w_hi) for j in range(IT)]:
                if zt is zt_lo and j == 0:
                    wait(pe, zl[s])
                mm = pe.matmul(banks[:, b, :], zt[:, s % 2, j, :], weights(s, w, 2048 + j * 512), start=(j == 0 and zt is zt_hi and w is w_hi),
                               stop=(j == IT - 1 and zt is zt_lo))
            dn[s] = c_pe.by(mm)

        def finish(s):
            kind, n = steps[s]
            r, b = s % 3, 6
            wait(act, dn[s])
            if s >= 3:
                wait(act, sent[s - 3])
            if kind == "shared":
                od[s] = c_act.by(act.copy(o_sb[:, r, :], banks[:, b, :]))
                wait(pool, add_ready[s], od[s])
                added[s] = c_pool.by(pool.tensor_tensor(o_sb[:, r, :], o_sb[:, r, :], add_in[:, s % 2, :], ALU.add))
                wait(nc.sync, added[s])
                sent[s] = c_st[r].by(nc.sync.dma_start(out[n * B:(n + 1) * B, :], o_sb[:, r, :]), 16)
                return
            wait(act, wtk[s])
            od[s] = c_act.by(act.activation(o_sb[:, r, :], banks[:, b, :], ACT.Copy, scale=w_tok[:, s % 4:s % 4 + 1]))
            wait(pool, od[s])
            if n == 0:
                wait(pool, marks["scatter"], m_init, *[sent[t] for t in range(H - 3, H)])
            else:
                wait(pool, scattered[-1])
            sent[s] = c_sa[r].by(pool.indirect_dma_start(
                out=out, out_offset=bass.IndirectOffsetOnAxis(ap=s_idx[:, n:n + 1], axis=0),
                in_=o_sb[:, r, :], in_offset=None, compute_op=ALU.add), 16)
            scattered.append(sent[s])

        for s in range(2):
            fetch(s)
        turn_rows(0)
        split_rows(0)
        for s in range(NS + 2):
            j = s - E0
            if j == -4:
                pull(1000)
            if "meta" in marks and not raw_in:
                for c in range(3):
                    job_fetch(-2, c)
                for c in range(3):
                    job_fetch(-1, c)
            fetch_addend(s - 1)
            if s + 2 < NS:
                fetch(s + 2)
            for c in range(3):
                if j + 2 - c >= 0:
                    job_fetch(j + 2 - c, c)
            if s < NS:
                up(s, 0)
            if j < -4:
                pull(PULL)
            if s + 1 < NS:
                turn_rows(s + 1)
            if j == -2:
                job_split(-2, 0), job_split(-2, 1), job_split(-2, 2)
            if j == -1:
                job_split(-1, 0), job_split(-1, 1)
            if s + 1 < NS:
                split_rows(s + 1)
            if s < NS:
                up(s, 1)
                activate(s)
            if 1 <= s <= NS:
                turn_z(s - 1)
                split_z(s - 1)
            if j == 0:
                job_split(-1, 2)
            if 0 <= j < 3:
                job_split(0, j)
            if j >= 0:
                jobs_split(dve, j)
            if s >= 2:
                down(s - 2)
                finish(s - 2)
            if j < -4:
                pull(PULL)
            if j >= 0:
                if j == 0:
                    wait(act, marks["meta"])
                jobs_split(act, j)
        wait(nc.sync, *[sent[s] for s in range(NS - 3, NS)])


def kernel(x, itok_B_78_3631, L0_cond_log_dt, L0_cond_C, L0_cond_log_A_real, L0_cond_A_imag, L0_cond_D,
           L0_ffn_gate_w, L0_ffn_bias, L0_ffn_Wg, L0_ffn_Wu, L0_ffn_Wd, L0_ffn_Sg, L0_ffn_Su, L0_ffn_Sd):
    import numpy as np
    import concourse.bacc as bacc
    from concourse.bass_utils import run_bass_kernel_spmd

    def a(v):
        return np.asarray(v)

    def k_major(w, rows):
        w = np.swapaxes(a(w), -1, -2)
        w = w.reshape(*w.shape[:-2], rows // P, P, w.shape[-1])
        return np.ascontiguousarray(np.swapaxes(w, -3, -2))

    def pack(wg, wu, wd):
        up = np.stack([k_major(wg, L), k_major(wu, L)], axis=-2)
        return np.concatenate([w.reshape(*w.shape[:w.ndim - k], -1) for w, k in ((up, 3), (k_major(wd, I), 2))], axis=-1)

    w_all = np.concatenate([pack(L0_ffn_Wg, L0_ffn_Wu, L0_ffn_Wd), pack(L0_ffn_Sg, L0_ffn_Su, L0_ffn_Sd)[None]])
    xn = a(x)
    arrays = {
        "x": np.ascontiguousarray(xn.transpose(1, 0, 2)).reshape(H * B, L),
        "xT": np.ascontiguousarray(xn.transpose(2, 1, 0).reshape(KT, P, H * B)[:, ::-1]),
        "lens": a(itok_B_78_3631).reshape(B, 1),
        "log_dt": a(L0_cond_log_dt).reshape(1, H),
        "c_re": np.ascontiguousarray(a(L0_cond_C)[..., 0].T),
        "c_im": np.ascontiguousarray(a(L0_cond_C)[..., 1].T),
        "log_a": np.ascontiguousarray(a(L0_cond_log_A_real).T),
        "a_im": np.ascontiguousarray(a(L0_cond_A_imag).T),
        "d_skip": a(L0_cond_D).reshape(1, H),
        "gate_w": k_major(L0_ffn_gate_w, L),
        "bias": a(L0_ffn_bias).reshape(1, E),
        "w_all": w_all,
    }
    nc = bacc.Bacc("TRN2", target_bir_lowering=False, num_devices=1)
    args = {}
    for name, arr in arrays.items():
        args[name] = nc.dram_tensor(name, arr.shape, mybir.dt.from_np(arr.dtype), kind="ExternalInput").ap()
    args["out"] = nc.dram_tensor("out", (H * B + P, L), F32, kind="ExternalOutput").ap()
    args["kpad"] = nc.dram_tensor("kpad", (H, KPITCH), F32).ap()
    args["yrow"] = nc.dram_tensor("yrow", (H * B, L + E), F32).ap()
    build(nc, **args)
    r = run_bass_kernel_spmd(nc, [arrays], core_ids=[0])
    return np.ascontiguousarray(r.results[0]["out"][0:H * B].reshape(H, B, L).transpose(1, 0, 2))
```
